# Optimizing a Trainium2 kernel written in Bass

```python
import numpy as np
import jax
import jax.numpy as jnp

def _softmax(x, axis=-1):
    return jax.nn.softmax(x, axis=axis)
def _gelu(x):
    return jax.nn.gelu(x, approximate=True)
def _silu(x):
    return jax.nn.silu(x)
def _sigmoid(x):
    return jax.nn.sigmoid(x)
def _layernorm(x, axis=-1, eps=1e-5):
    m = jnp.mean(x, axis=axis, keepdims=True)
    v = jnp.var(x, axis=axis, keepdims=True)
    return (x - m) / jnp.sqrt(v + eps)
def _scatter_add(tgt, idx, src, axis=0):
    return tgt.at[idx].add(src)
def _segment_sum(src, seg, n):
    return jax.ops.segment_sum(src, seg, n)

kernel_name = 'mk_adj_preln_d1_adj_256_ce24c2'

def setup_inputs(seed: int = 0):
    np.random.seed(seed)
    _w = jnp.asarray
    def _rec_inputs():
        import jax
        import jax.numpy as jnp
        _gk = jax.random.key(seed)
        x = -0.000929 + 1 * jax.random.normal(jax.random.fold_in(_gk, 1), (8192, 256), jnp.float32)
        _a = jax.random.bernoulli(jax.random.fold_in(_gk, 2), 0.000488281, (8192, 8192))
        adj = _a.astype(jnp.int32)
        return x, adj
    x, adj = _rec_inputs()
    def _L0_gnn_setup():
        import jax, jax.numpy as jnp
        import numpy as np
        N, IN_F, H, D = (4096, 256, 4, 64)
        NEG_SLOPE = 0.2
        key = jax.random.key(seed)
        ks = jax.random.split(key, 8)
        s_w = 1.0 / np.sqrt(H * D)
        s_u = 1.0
        return {'inputs': jax.random.normal(ks[0], (N, IN_F), jnp.float32), 'adj_mat': jax.random.randint(ks[1], (N, N), 0, 2, jnp.int32), 'weight': jax.random.normal(ks[2], (IN_F, H * D), jnp.float32) * s_w, 'weight_u': jax.random.normal(ks[3], (H, D, 1), jnp.float32) * s_u, 'weight_v': jax.random.normal(ks[4], (H, D, 1), jnp.float32) * s_u, 'bias': jax.random.normal(ks[5], (1, H * D), jnp.float32) * s_w, 'proj_w': jax.random.normal(ks[6], (H * D, IN_F), jnp.float32) * (1.0 / np.sqrt(IN_F)), 'proj_b': jax.random.normal(ks[7], (H * D,), jnp.float32) * (1.0 / np.sqrt(IN_F))}
    _L0_gnn_all = _L0_gnn_setup()
    _L0_gnn_in = {k: v for k, v in _L0_gnn_all.items() if k in ('weight', 'weight_u', 'weight_v', 'bias', 'proj_w', 'proj_b', )}
    del _L0_gnn_all

    return {
        "x": x,
        "adj": adj,
        "L0_gnn_weight": _L0_gnn_in["weight"],
        "L0_gnn_weight_u": _L0_gnn_in["weight_u"],
        "L0_gnn_weight_v": _L0_gnn_in["weight_v"],
        "L0_gnn_bias": _L0_gnn_in["bias"],
        "L0_gnn_proj_w": _L0_gnn_in["proj_w"],
        "L0_gnn_proj_b": _L0_gnn_in["proj_b"],
    }

def reference(x, adj, L0_gnn_weight, L0_gnn_weight_u, L0_gnn_weight_v, L0_gnn_bias, L0_gnn_proj_w, L0_gnn_proj_b):
    import jax
    import jax.numpy as jnp
    def _L0_gnn_ref(inputs, adj_mat, weight, weight_u, weight_v, bias, proj_w, proj_b):
        import jax, jax.numpy as jnp
        import numpy as np
        N, IN_F, H, D = (4096, 256, 4, 64)
        NEG_SLOPE = 0.2
        support = (inputs @ weight).reshape(-1, H, D).transpose(1, 0, 2)
        f1 = jnp.einsum('hnd,hd->hn', support, weight_u[..., 0])[:, None, :]
        f2 = jnp.einsum('hnd,hd->hn', support, weight_v[..., 0])[:, :, None]
        scores = jax.nn.leaky_relu(f1 + f2, NEG_SLOPE)
        masked = scores * adj_mat.astype(scores.dtype)
        mask = masked != 0
        neg_inf = jnp.asarray(-jnp.inf, masked.dtype)
        m = jnp.max(jnp.where(mask, masked, neg_inf), axis=2, keepdims=True)
        m = jnp.where(jnp.isfinite(m), m, jnp.zeros_like(m))
        e = jnp.where(mask, jnp.exp(masked - m), jnp.zeros_like(masked))
        denom = e.sum(axis=2, keepdims=True)
        attn = jnp.where(denom > 0, e / jnp.where(denom > 0, denom, 1.0), jnp.zeros_like(e))
        out = jnp.einsum('hnm,hmd->hnd', attn, support)
        out = out.transpose(1, 0, 2).reshape(-1, H * D)
        out = out + bias
        out = out + inputs @ proj_w.T + proj_b
        return out

    h = jnp.maximum(_layernorm(x, axis=-1), 0.0)
    x = x + _L0_gnn_ref(h, adj, L0_gnn_weight, L0_gnn_weight_u, L0_gnn_weight_v, L0_gnn_bias, L0_gnn_proj_w, L0_gnn_proj_b)
    return x


_drawn_inputs = setup_inputs


def setup_inputs(seed=0):
    import zlib

    import numpy as np

    out = dict(_drawn_inputs(seed))
    spreads = {}
    factors = {}
    for name, (base, spread) in spreads.items():
        noise = np.random.default_rng([zlib.crc32(name.encode()), seed]).standard_normal(out[name].shape)
        drawn = base * np.exp(spread * noise) if base else spread * noise
        out[name] = jnp.asarray(drawn.astype(out[name].dtype))
    for name, factor in factors.items():
        out[name] = (out[name] * factor).astype(out[name].dtype)
    return out
```

```python
from contextlib import ExitStack

import concourse.bass as bass
from concourse import mybir

ALU = mybir.AluOpType
ACT = mybir.ActivationFunctionType
F32 = mybir.dt.float32
BF16 = mybir.dt.bfloat16
I32 = mybir.dt.int32
U32 = mybir.dt.uint32
AX_X = mybir.AxisListType.X

P = 128
SLOTS = 16
BITS = 8
RING = 4
GROUP = 4
EMPTY = float(2 ** 20)
NEG = -1e30
SLOPE = 0.2
EPS = 1e-5


def gat_kernel(nc, x, adj, weight, weight_u, weight_v, bias, proj_wT, proj_b, out):
    N, D = x.shape
    H, HD = weight_u.shape[0], weight_u.shape[1]
    HF = H * HD
    KC = D // P
    TILES = N // P
    WORDS = N // BITS
    ROWS_STEP = P // BITS
    UNITS = 4
    UT = BITS // UNITS
    BANKS = WORDS // 512
    CANDS = 64
    SEG = WORDS // (CANDS // 8)
    ROW = HF + H
    STAGE = 2 * HF + 2 * H

    with ExitStack() as ctx:
        def sb(name, shape, dt=F32):
            return ctx.enter_context(nc.sbuf_tensor(name, shape, dt))

        def sem(name):
            return ctx.enter_context(nc.semaphore(name))

        table = nc.dram_tensor("support_table", (N, ROW), F32, kind="Internal").ap()

        adj_raw = sb("adj_raw", [P, UNITS, UT, WORDS], I32)
        adj_bf = sb("adj_bf", [P, UNITS, UT, WORDS], BF16)
        gathered = sb("gathered", [P, RING, SLOTS * ROW])
        base = sb("base", [P, TILES, HF])
        node = sb("node", [P, TILES, 2 * H])
        out_tile = sb("out_tile", [P, RING, HF])
        ident = sb("ident", [P, P])
        ones_f = sb("ones_f", [P, P])
        w_all = sb("w_all", [P, KC, 2 * HF])
        w_uv = sb("w_uv", [P, KC, 2 * H])
        uv_row = sb("uv_row", [P, 2, HF])
        bias_row = sb("bias_row", [P, HF])
        projb_row = sb("projb_row", [P, HF])
        hT = sb("hT", [P, 2, KC * P])
        stats = sb("stats", [P, GROUP, 6])
        mean_var = sb("mean_var", [P, GROUP, 2])
        std = sb("std", [P, GROUP])
        rstd = sb("rstd", [P, GROUP])
        eps_col = sb("eps_col", [P, 1])
        pack_w = sb("pack_w", [P, BITS, P], BF16)
        pack_i = sb("pack_i", [P, 1], I32)
        pack_f = sb("pack_f", [P, 1])
        pack_blk = sb("pack_blk", [P, ROWS_STEP])
        ones_row = sb("ones_row", [1, P], BF16)
        place_lo = sb("place_lo", [1, WORDS], BF16)
        place_hi = sb("place_hi", [1, WORDS], BF16)
        bit_shift = sb("bit_shift", [P, BITS], I32)
        bit_first = sb("bit_first", [P, BITS])
        cand = sb("cand", [P, CANDS])
        cand_rest = sb("cand_rest", [P, CANDS])
        words = sb("words", [P, SLOTS])
        words_i = sb("words_i", [P, SLOTS], I32)
        place_i = sb("place_i", [P, SLOTS], I32)
        bits = sb("bits", [P, SLOTS, BITS], I32)
        codes = sb("codes", [P, SLOTS, BITS])
        codes_rest = sb("codes_rest", [P, SLOTS * BITS])
        nbr = sb("nbr", [P, SLOTS])
        empty = sb("empty", [P, RING, SLOTS])
        idx = sb("idx", [P, RING, SLOTS], U32)
        score = sb("score", [P, SLOTS, H])
        zero_pen = sb("zero_pen", [P, SLOTS, H])
        row_max = sb("row_max", [P, H])
        row_ref = sb("row_ref", [P, H])
        shifted = sb("shifted", [P, RING, SLOTS * H])
        expd = sb("expd", [P, RING, SLOTS * H])
        denom = sb("denom", [P, H])
        denom1 = sb("denom1", [P, H])
        rdenom = sb("rdenom", [P, H])
        prob = sb("prob", [P, SLOTS, H])
        adj_sum = sb("adj_sum", [P, TILES * UNITS])
        empty_sum = sb("empty_sum", [P, SLOTS])

        x_in_ap = gathered[:, 2, 0:2 * GROUP * D].rearrange("p (b i d) -> p b i d", b=2, i=GROUP)
        xhat = gathered[:, 2, 2 * GROUP * D:4 * GROUP * D].rearrange("p (b i d) -> p b i d", b=2, i=GROUP)
        stage = gathered[:, 3, 0:2 * GROUP * STAGE].rearrange("p (b i d) -> p b i d", b=2, i=GROUP)

        ps_words = ctx.enter_context(nc.psum_tensor("ps_words", [P, 2, WORDS], F32))
        ps_out = ctx.enter_context(nc.psum_tensor("ps_out", [P, 2, 512], F32))
        ps_t = ctx.enter_context(nc.psum_tensor("ps_t", [P, 2, 512], F32))

        s_w_in = sem("weights_in")
        s_uv = sem("weight_uv_ready")
        s_pool_const = sem("pool_constants")
        s_dve_const = sem("dve_constants")
        s_x_in = [sem(f"x_in{b}") for b in range(2)]
        s_stats = sem("stats_ready")
        s_std = sem("std_ready")
        s_norm = sem("norm_chain")
        s_xhat = sem("xhat_ready")
        s_xT = sem("xT_ready")
        s_hT = sem("hT_ready")
        s_proj = sem("projected")
        s_staged = sem("staged")
        s_basev = sem("base_partial")
        s_based = sem("base_ready")
        s_rows_out = [sem(f"table_rows_out{b}") for b in range(2)]
        s_adj_in = [sem(f"adj_in{u}") for u in range(UNITS)]
        s_conv = sem("converted")
        s_adj_used = sem("adj_bf_used")
        s_words = sem("words_ready")
        s_words_read = sem("words_read")
        s_ex = sem("extract_chain")
        s_idx = sem("idx_ready")
        s_gather = [sem(f"rows_gathered{b}") for b in range(RING)]
        s_sc = sem("score_chain")
        s_shifted = sem("shifted_ready")
        s_exp = sem("exp_ready")
        s_pr = sem("prob_chain")
        s_weighted = sem("weighted_ready")
        s_reduced = sem("reduced")
        s_out = sem("out_ready")
        s_stored = [sem(f"out_stored{b}") for b in range(RING)]

        s_gate_dve = sem("gate_dve")
        s_gate_pool = sem("gate_pool")

        s_check = sem("check_chain")
        s_missed = sem("missed_summed")
        s_flag = sem("flag_ready")
        d_init = sem("dense_tile_ready")
        d_adj_in = sem("dense_adj_in")
        d_diag = sem("dense_f1_diagonal")
        d_f1 = sem("dense_f1_spread")
        d_chain = [sem("dense_max_chain"), sem("dense_sum_chain")]
        d_shift = sem("dense_shifted")
        d_exp = sem("dense_exp")
        d_expT = sem("dense_exp_transposed")
        d_expT_sb = sem("dense_exp_transposed_in_sbuf")
        d_sup_in = sem("dense_support_in")
        d_part = sem("dense_partial_product")
        d_acc = sem("dense_accumulated")
        d_tail = sem("dense_tail_chain")
        d_out = sem("dense_out_ready")
        d_stored = sem("dense_out_stored")

        missed = sb("missed", [P, 4])
        flag = sb("flag", [1, 1], I32)
        dn_adj = adj_raw[:].rearrange("p u s e -> p (u s e)")
        dn = gathered[:, 0, :]
        dn_adjf = dn[:, 0:P]
        dn_diag, dn_s, dn_zero, dn_e, dn_eT = (
            dn[:, P + q * H * P:P + (q + 1) * H * P].rearrange("p (h m) -> p h m", h=H) for q in range(5))
        dn_acc = gathered[:, 1, 0:HF]
        dn_sup = gathered[:, 1, HF:2 * HF]
        dn_max, dn_part, dn_ref, dn_den, dn_rden = (
            gathered[:, 1, 2 * HF + q * H:2 * HF + (q + 1) * H] for q in range(5))
        ps_f1 = ps_words[:, 0, 0:H * P].rearrange("p (h m) -> p h m", h=H)
        ps_eT = ps_words[:, 1, 0:H * P].rearrange("p (h m) -> p h m", h=H)

        adj_v = adj.rearrange("(T u s n) (m e) -> T u (n m) s e", u=UNITS, s=UT, n=ROWS_STEP, m=BITS)
        x_v = x.rearrange("(g i p) d -> g p i d", i=GROUP, p=P)
        table_v = table.rearrange("(g i p) d -> g p i d", i=GROUP, p=P)
        out_v = out.rearrange("(t p) d -> t p d", p=P)
        adj_rows = adj.rearrange("(t p) m -> t p m", p=P)
        table_rows = table[:, 0:HF].rearrange("(t p) d -> t p d", p=P)
        GROUPS = TILES // GROUP

        block = ctx.enter_context(nc.Block())

        @block.sync
        def _(sp):
            for c in range(KC):
                sp.dma_start(w_all[:, c, 0:HF], proj_wT[c * P:(c + 1) * P, :]).then_inc(s_w_in, 16)
                sp.dma_start(w_all[:, c, HF:], weight[c * P:(c + 1) * P, :]).then_inc(s_w_in, 16)
            for dst, src in ((uv_row[:, 0, :], weight_u.rearrange("h d o -> o (h d)")),
                             (uv_row[:, 1, :], weight_v.rearrange("h d o -> o (h d)")),
                             (bias_row[:, :], bias),
                             (projb_row[:, :], proj_b.rearrange("(o d) -> o d", o=1))):
                sp.dma_start(dst, src.to_broadcast([P, HF])).then_inc(s_w_in, 16)

            def load_x(j, b, first):
                g = 2 * j + b
                if not first:
                    sp.wait_ge(s_xhat, GROUP * (g - 1))
                    sp.wait_ge(s_based, GROUP * (g - 1))
                sp.dma_start(x_in_ap[:, b], x_v[g]).then_inc(s_x_in[b], 16)

            def load_adj(j, b, first):
                t = RING * j + b
                for u in range(UNITS):
                    if not (first and b == 0):
                        sp.wait_ge(s_conv, UNITS * (t - 1) + u + 1)
                    sp.dma_start(adj_raw[:, u], adj_v[t, u]).then_inc(s_adj_in[u], 16)

            def store_out(j, b):
                t = RING * j + b
                sp.wait_ge(s_out, t + 1)
                sp.dma_start(out_v[t], out_tile[:, b, :]).then_inc(s_stored[b], 16)

            load_x(0, 0, True)
            load_x(0, 1, True)
            load_adj(0, 0, True)
            with sp.Fori(1, GROUPS // 2) as j:
                load_x(j, 0, False)
                load_x(j, 1, False)
            for b in range(1, RING):
                load_adj(0, b, True)
            with sp.Fori(1, TILES // RING) as j:
                for b in range(RING):
                    load_adj(j, b, False)
                    store_out(j - 1, b)
            for b in range(RING):
                store_out(TILES // RING - 1, b)
            for b in range(RING):
                sp.wait_ge(s_stored[b], 16 * (TILES // RING))

            sp.wait_ge(s_flag, 1)
            with sp.If(sp.value_load(flag[0:1, 0:1], min_val=0, max_val=1) > 0):
                with sp.Fori(0, TILES) as i:
                    sp.wait_ge(d_init, i + 1)
                    sp.dma_start(dn_adj, adj_rows[i]).then_inc(d_adj_in, 16)
                    with sp.Fori(0, TILES) as c:
                        sp.wait_ge(d_acc, TILES * i + c + i + 1)
                        sp.dma_start(dn_sup, table_rows[c]).then_inc(d_sup_in, 16)
                    sp.wait_ge(d_out, i + 1)
                    sp.dma_start(out_v[i], out_tile[:, 0, :]).then_inc(d_stored, 16)
                sp.wait_ge(d_stored, 16 * TILES)

        @block.tensor
        def _(pe):
            def transposes(t, b, first):
                pe.wait_ge(s_xhat, t + 1)
                if not first:
                    pe.wait_ge(s_hT, t - 1)
                for c in range(KC):
                    mm = nc.tensor.transpose(ps_t[:, b % 2, c * P:(c + 1) * P],
                                             xhat[:, b // GROUP, b % GROUP, c * P:(c + 1) * P], ident[:])
                mm.then_inc(s_xT, 1)

            def project(t, b, first):
                pe.wait_ge(s_hT, t + 1)
                if not first:
                    pe.wait_ge(s_staged, t - 1)
                for c in range(KC):
                    nc.tensor.matmul(ps_out[:, b % 2, :], hT[:, b % 2, c * P:(c + 1) * P], w_all[:, c, :],
                                     start=(c == 0), stop=(c == KC - 1))
                for c in range(KC):
                    mm = nc.tensor.matmul(ps_words[:, b % 2, 0:2 * H], hT[:, b % 2, c * P:(c + 1) * P],
                                          w_uv[:, c, :], start=(c == 0), stop=(c == KC - 1))
                mm.then_inc(s_proj, 1)

            pe.wait_ge(s_pool_const, 4)
            pe.wait_ge(s_w_in, 16 * (2 * KC + 4))
            pe.wait_ge(s_uv, 4)

            def phase_a(j, first):
                for gb in range(2):
                    for i in range(GROUP + 1):
                        b = gb * GROUP + i
                        if i < GROUP:
                            transposes(2 * GROUP * j + b, b, first and b < 2)
                        if i > 0:
                            project(2 * GROUP * j + b - 1, b - 1, first and b - 1 < 2)

            phase_a(0, True)
            with pe.Fori(1, GROUPS // 2) as j:
                phase_a(j, False)

            def pack(j, b, first):
                t = RING * j + b
                if not (first and b < 2):
                    pe.wait_ge(s_words_read, t - 1)
                for k in range(BANKS):
                    o = ps_words[:, b % 2, k * 512:(k + 1) * 512]
                    for row in (place_lo, place_hi):
                        nc.tensor.matmul(o, ones_row[:], row[:, k * 512:(k + 1) * 512],
                                         start=(row is place_lo), stop=False)
                for u in range(UNITS):
                    pe.wait_ge(s_conv, UNITS * t + u + 1)
                    for s in range(UT):
                        for k in range(BANKS):
                            mm = nc.tensor.matmul(ps_words[:, b % 2, k * 512:(k + 1) * 512],
                                                  pack_w[:, u * UT + s, :],
                                                  adj_bf[:, u, s, k * 512:(k + 1) * 512],
                                                  start=False, stop=(u == UNITS - 1 and s == UT - 1))
                    mm.then_inc(s_adj_used, 1)

            def reduce_slots(j, b, first):
                t = RING * j + b
                pe.wait_ge(s_weighted, t + 1)
                if not (first and b < 2):
                    pe.wait_ge(s_out, t - 1)
                g = gathered[:, b, :].rearrange("p (k r) -> p k r", k=SLOTS)
                for k in range(SLOTS):
                    mm = nc.tensor.matmul(ps_out[:, b % 2, 0:HF], ident[:], g[:, k, 0:HF],
                                          start=(k == 0), stop=(k == SLOTS - 1))
                mm.then_inc(s_reduced, 1)

            pe.wait_ge(s_staged, TILES)
            pe.wait_ge(s_dve_const, 8)

            def body(j, first):
                for b in range(RING):
                    pack(j, b, first)
                    if b >= 3:
                        reduce_slots(j, b - 3, first)
                    elif not first:
                        reduce_slots(j - 1, b + 1, False)

            body(0, True)
            body(1, False) if TILES // RING == 1 else None
            with pe.Fori(1, TILES // RING) as j:
                body(j, False)
            for b in range(1, RING):
                reduce_slots(TILES // RING - 1, b, False)

            pe.wait_ge(s_check, 4)
            nc.tensor.matmul(ps_out[0:1, 0, 0:1], missed[:, 3:4], ones_f[:, 0:1], start=True,
                             stop=True).then_inc(s_missed, 1)
            pe.wait_ge(s_flag, 1)
            with pe.If(pe.value_load(flag[0:1, 0:1], min_val=0, max_val=1) > 0):
                def spread_f1(n):
                    pe.wait_ge(d_diag, n + 1)
                    nc.tensor.matmul(ps_f1, ones_f[:], dn_diag, start=True, stop=True).then_inc(d_f1, 1)

                with pe.Fori(0, TILES) as i:
                    with pe.Fori(0, TILES) as c:
                        spread_f1(2 * TILES * i + c)
                    with pe.Fori(0, TILES) as c:
                        spread_f1(2 * TILES * i + TILES + c)
                        pe.wait_ge(d_exp, TILES * i + c + 1)
                        for h in range(H):
                            mm = nc.tensor.transpose(ps_eT[:, h, :], dn_e[:, h, :], ident[:])
                        mm.then_inc(d_expT, 1)
                        pe.wait_ge(d_sup_in, 16 * (TILES * i + c + 1))
                        pe.wait_ge(d_expT_sb, TILES * i + c + 1)
                        for h in range(H):
                            mm = nc.tensor.matmul(ps_out[:, 0, h * HD:(h + 1) * HD], dn_eT[:, h, :],
                                                  dn_sup[:, h * HD:(h + 1) * HD], start=True, stop=True)
                        mm.then_inc(d_part, 1)

        @block.scalar
        def _(act):
            def phase_a(j, first):
                for gb in range(2):
                    g = 2 * j + gb
                    act.wait_ge(s_stats, g + 1)
                    nc.scalar.activation(std[:], mean_var[:, :, 1], ACT.Sqrt, bias=eps_col[:, 0:1]).then_inc(s_std, 1)
                    if not first:
                        act.wait_ge(s_based, GROUP * (g - 1))
                        act.wait_ge(s_rows_out[gb], 16 * j)
                    for i in range(GROUP + 1):
                        b = gb * GROUP + i
                        t = 2 * GROUP * j + b
                        if i < GROUP:
                            act.wait_ge(s_xT, t + 1)
                            if not (first and b < 2):
                                act.wait_ge(s_proj, t - 1)
                            nc.scalar.activation(hT[:, b % 2, :], ps_t[:, b % 2, 0:KC * P],
                                                 ACT.Relu).then_inc(s_hT, 1)
                        if i > 0:
                            act.wait_ge(s_proj, t)
                            nc.scalar.activation(stage[:, gb, i - 1, 0:2 * HF], ps_out[:, (b - 1) % 2, :],
                                                 ACT.Copy)
                            nc.scalar.activation(stage[:, gb, i - 1, 2 * HF:STAGE],
                                                 ps_words[:, (b - 1) % 2, 0:2 * H],
                                                 ACT.Copy).then_inc(s_staged, 1)
                    act.wait_ge(s_staged, GROUP * (g + 1))
                    act.dma_start(table_v[g], stage[:, gb, :, HF:HF + ROW]).then_inc(s_rows_out[gb], 16)

            act.wait_ge(s_dve_const, 8)
            phase_a(0, True)
            with act.Fori(1, GROUPS // 2) as j:
                phase_a(j, False)

            def convert(j, b, first):
                t = RING * j + b
                for u in range(UNITS):
                    act.wait_ge(s_adj_in[u], 16 * (t + 1))
                    if not (first and b == 0):
                        act.wait_ge(s_adj_used, UNITS * (t - 1) + u + 1)
                    nc.scalar.activation(adj_bf[:, u], adj_raw[:, u], ACT.Copy,
                                         accum_out=adj_sum[:, bass.ds(UNITS * t + u, 1)]).then_inc(s_conv, 1)

            def exponential(j, b):
                t = RING * j + b
                act.wait_ge(s_shifted, t + 1)
                nc.scalar.activation(expd[:, b, :], shifted[:, b, :], ACT.Exp).then_inc(s_exp, 1)

            def body(j, first):
                for b in range(RING):
                    convert(j, b, first)
                    if b >= 2:
                        exponential(j, b - 2)
                    elif not first:
                        exponential(j - 1, b + 2)

            body(0, True)
            with act.Fori(1, TILES // RING) as j:
                body(j, False)
            for b in range(2, RING):
                exponential(TILES // RING - 1, b)

            act.wait_ge(s_flag, 1)
            with act.If(act.value_load(flag[0:1, 0:1], min_val=0, max_val=1) > 0):
                with act.Fori(0, TILES * TILES) as n:
                    act.wait_ge(d_shift, n + 1)
                    nc.scalar.activation(dn_e, dn_s, ACT.Exp).then_inc(d_exp, 1)
                    act.wait_ge(d_expT, n + 1)
                    nc.scalar.activation(dn_eT, ps_eT, ACT.Copy).then_inc(d_expT_sb, 1)

        @block.gpsimd
        def _(pool):
            pool.memset(ident[:], 0.0).then_inc(s_pool_const, 1)
            pool.memset(pack_blk[:], 1.0).then_inc(s_pool_const, 1)
            pool.wait_ge(s_pool_const, 2)
            pool.affine_select(ident[:], ident[:], [[-1, P]], ALU.not_equal, 1.0, base=0,
                               channel_multiplier=1).then_inc(s_pool_const, 1)
            pool.affine_select(pack_blk[:], pack_blk[:], [[-BITS, ROWS_STEP]], ALU.is_ge, 0.0, base=0,
                               channel_multiplier=1).then_inc(s_pool_const, 1)
            pool.wait_ge(s_pool_const, 4)
            pool.affine_select(pack_blk[:], pack_blk[:], [[BITS, ROWS_STEP]], ALU.is_ge, 0.0, base=BITS - 1,
                               channel_multiplier=-1).then_inc(s_pool_const, 1)
            pool.iota(pack_i[:], [[0, 1]], base=0, channel_multiplier=1).then_inc(s_pool_const, 1)
            pool.iota(place_lo[:], [[0, WORDS // 256], [1, 256]], base=0, channel_multiplier=0,
                      allow_small_or_imprecise_dtypes=True).then_inc(s_pool_const, 1)
            pool.iota(place_hi[:], [[256, WORDS // 256], [0, 256]], base=0, channel_multiplier=0,
                      allow_small_or_imprecise_dtypes=True).then_inc(s_pool_const, 1)
            pool.iota(bit_shift[:], [[1, BITS]], base=WORDS.bit_length() - 1,
                      channel_multiplier=0).then_inc(s_pool_const, 1)
            pool.iota(bit_first[:], [[WORDS, BITS]], base=1, channel_multiplier=0,
                      allow_small_or_imprecise_dtypes=True).then_inc(s_pool_const, 1)
            pool.memset(gathered[:, 0, :], 0.0).then_inc(s_pool_const, 1)
            pool.memset(gathered[:, 1, :], 0.0).then_inc(s_pool_const, 1)
            pool.memset(gathered[:, 2, 4 * GROUP * D:], 0.0).then_inc(s_pool_const, 1)
            pool.wait_ge(s_w_in, 16 * (2 * KC + 4))
            pool.tensor_tensor(bias_row[:], bias_row[:], projb_row[:], ALU.add).then_inc(s_pool_const, 1)
            pool.wait_ge(s_pool_const, 14)

            def phase_a(j, first):
                for gb in range(2):
                    pool.wait_ge(s_x_in[gb], 16 * (j + 1))
                    for i in range(GROUP):
                        t = GROUP * (2 * j + gb) + i
                        bt = base[:, bass.ds(t, 1), :].rearrange("p o d -> p (o d)")
                        pool.tensor_tensor(bt, x_in_ap[:, gb, i, :], bias_row[:], ALU.add).then_inc(s_basev, 1)
                        pool.wait_ge(s_staged, t + 1)
                        pool.wait_ge(s_basev, t + 1)
                        pool.tensor_copy(node[:, bass.ds(t, 1), :].rearrange("p o d -> p (o d)"),
                                         stage[:, gb, i, 2 * HF:STAGE])
                        pool.tensor_tensor(bt, bt, stage[:, gb, i, 0:HF], ALU.add).then_inc(s_based, 1)

            phase_a(0, True)
            with pool.Fori(1, GROUPS // 2) as j:
                phase_a(j, False)

            for b in range(2):
                pool.wait_ge(s_rows_out[b], 16 * (GROUPS // 2))

            def gather(j, b, first):
                t = RING * j + b
                pool.wait_ge(s_idx, t + 1)
                if not first:
                    pool.wait_ge(s_reduced, t - RING + 1)
                    pool.sem_inc(s_gate_pool)
                g = gathered[:, b, :].rearrange("p (k r) -> p k r", k=SLOTS)
                for k in range(SLOTS):
                    pool.indirect_dma_start(g[:, k, :], None, table, bass.IndirectOffsetOnAxis(idx[:, b, k:k + 1], 0),
                                            bounds_check=N - 1, oob_is_err=False).then_inc(s_gather[b], 16)

            for b in range(RING):
                gather(0, b, True)
            with pool.Fori(1, TILES // RING) as j:
                for b in range(RING):
                    gather(j, b, False)

        @block.vector
        def _(dve):
            v = nc.vector
            v.memset(eps_col[:], EPS).then_inc(s_dve_const, 1)
            v.memset(ones_f[:], 1.0).then_inc(s_dve_const, 1)
            v.memset(ones_row[:], 1.0).then_inc(s_dve_const, 1)
            v.memset(empty_sum[:], 0.0).then_inc(s_dve_const, 1)
            v.memset(pack_w[:], 0.0).then_inc(s_dve_const, 1)
            dve.wait_ge(s_pool_const, 13)
            v.tensor_single_scalar(pack_i[:], pack_i[:], BITS - 1, ALU.bitwise_and).then_inc(s_dve_const, 1)
            dve.wait_ge(s_dve_const, 6)
            v.tensor_single_scalar(pack_i[:], pack_i[:], 127 + WORDS.bit_length() - 1, ALU.add).then_inc(s_dve_const, 1)
            dve.wait_ge(s_dve_const, 7)
            v.tensor_single_scalar(pack_i[:], pack_i[:], 23, ALU.logical_shift_left).then_inc(s_norm, 1)
            dve.wait_ge(s_norm, 1)
            for s in range(BITS):
                last = v.tensor_scalar(pack_w[:, s, s * ROWS_STEP:(s + 1) * ROWS_STEP], pack_blk[:],
                                       pack_i[:].bitcast(F32)[:, 0:1], None, ALU.mult)
            last.then_inc(s_dve_const, 1)
            dve.wait_ge(s_w_in, 16 * (2 * KC + 4))
            tmp = gathered[:, 0, 0:2 * KC * HF].rearrange("p (q c d) -> p q c d", q=2, c=KC)
            dve.wait_ge(s_pool_const, 14)
            for q in range(2):
                for c in range(KC):
                    v.tensor_tensor(tmp[:, q, c], w_all[:, c, HF:], uv_row[:, q, :], ALU.mult).then_inc(s_norm, 1)
            dve.wait_ge(s_norm, 1 + 2 * KC)
            for q in range(2):
                for c in range(KC):
                    v.tensor_reduce(w_uv[:, c, q * H:(q + 1) * H],
                                    tmp[:, q, c].rearrange("p (h d) -> p h d", h=H), AX_X, ALU.add).then_inc(s_uv, 1)

            def phase_a(j, first):
                for gb in range(2):
                    g = 2 * j + gb
                    dve.wait_ge(s_x_in[gb], 16 * (j + 1))
                    for i in range(GROUP):
                        last = v.bn_stats(stats[:, i, :], x_in_ap[:, gb, i, :])
                    last.then_inc(s_bn, 1)
                    dve.wait_ge(s_bn, g + 1)
                    dve.sem_inc(s_gate_dve)
                    for i in range(GROUP):
                        last = v.bn_aggr(mean_var[:, i, :], stats[:, i, :])
                    last.then_inc(s_stats, 1)
                    dve.wait_ge(s_stats, g + 1)
                    dve.wait_ge(s_std, g + 1)
                    v.reciprocal(rstd[:], std[:]).then_inc(s_rstd, 1)
                    dve.wait_ge(s_rstd, g + 1)
                    for i in range(GROUP):
                        t = GROUP * g + i
                        if not first:
                            dve.wait_ge(s_xT, t + 1 - 2 * GROUP)
                        v.tensor_scalar(xhat[:, gb, i, :], x_in_ap[:, gb, i, :], mean_var[:, i, 0:1],
                                        rstd[:, i:i + 1], ALU.subtract, ALU.mult).then_inc(s_xhat, 1)

            s_bn = sem("bn_stats_done")
            s_rstd = sem("rstd_ready")
            phase_a(0, True)
            with dve.Fori(1, GROUPS // 2) as j:
                phase_a(j, False)
            dve.wait_ge(s_based, TILES)

            EX = 10

            def extract(j, b, first):
                t = RING * j + b
                n = [0]

                def link(ins):
                    n[0] += 1
                    ins.then_inc(s_ex, 1)
                    dve.wait_ge(s_ex, EX * t + n[0])
                    dve.sem_inc(s_gate_dve)

                dve.wait_ge(s_adj_used, UNITS * (t + 1))
                dve.sem_inc(s_gate_dve)
                for s in range(CANDS // 8):
                    last = v.max(cand[:, s * 8:(s + 1) * 8], ps_words[:, b % 2, s * SEG:(s + 1) * SEG])
                last.then_inc(s_words_read, 1)
                dve.wait_ge(s_words_read, t + 1)
                dve.sem_inc(s_gate_dve)
                link(v.max(words[:, 0:8], cand[:]))
                link(v.match_replace(cand_rest[:], words[:, 0:8], cand[:], 0.0))
                link(v.max(words[:, 8:16], cand_rest[:]))
                link(v.tensor_copy(words_i[:], words[:]))
                v.tensor_tensor(bits[:], words_i[:].unsqueeze(2).to_broadcast([P, SLOTS, BITS]),
                                bit_shift[:].unsqueeze(1).to_broadcast([P, SLOTS, BITS]), ALU.logical_shift_right)
                link(v.tensor_single_scalar(place_i[:], words_i[:], WORDS - 1, ALU.bitwise_and))
                v.tensor_tensor(codes[:], place_i[:].unsqueeze(2).to_broadcast([P, SLOTS, BITS]),
                                bit_first[:].unsqueeze(1).to_broadcast([P, SLOTS, BITS]), ALU.add)
                link(v.tensor_single_scalar(bits[:], bits[:], 1, ALU.bitwise_and))
                link(v.tensor_tensor(codes[:], codes[:], bits[:], ALU.mult))
                codes_f = codes[:].rearrange("p k b -> p (k b)")
                link(v.max(nbr[:, 0:8], codes_f))
                link(v.match_replace(codes_rest[:], nbr[:, 0:8], codes_f, 0.0))
                link(v.max(nbr[:, 8:16], codes_rest[:]))
                assert n[0] == EX
                v.tensor_scalar(empty[:, b, :], nbr[:], 0.0, EMPTY, ALU.is_equal, ALU.mult).then_inc(s_empty, 1)
                dve.wait_ge(s_empty, t + 1)
                v.tensor_tensor(empty_sum[:], empty_sum[:], empty[:, b, :], ALU.add)
                v.scalar_tensor_tensor(idx[:, b, :], nbr[:], -1.0, empty[:, b, :], ALU.add,
                                       ALU.add).then_inc(s_idx, 1)

            s_empty = sem("empty_ready")
            SC = 7

            def scores(j, b):
                t = RING * j + b
                n = [0]

                def link(ins):
                    n[0] += 1
                    ins.then_inc(s_sc, 1)
                    dve.wait_ge(s_sc, SC * t + n[0])

                dve.wait_ge(s_gather[b], 16 * SLOTS * (j + 1))
                g = gathered[:, b, :].rearrange("p (k r) -> p k r", k=SLOTS)
                f2 = node[:, bass.ds(t, 1), H:].to_broadcast([P, SLOTS, H])
                link(v.tensor_tensor(score[:], g[:, :, HF:], f2, ALU.add))
                link(v.scalar_tensor_tensor(score[:], score[:], SLOPE, score[:], ALU.mult, ALU.max))
                link(v.tensor_scalar(zero_pen[:], score[:], 0.0, NEG, ALU.is_equal, ALU.mult))
                link(v.tensor_tensor(score[:], score[:], zero_pen[:], ALU.add))
                link(v.scalar_tensor_tensor(score[:], empty[:, b, :].unsqueeze(2).to_broadcast([P, SLOTS, H]),
                                            NEG / EMPTY, score[:], ALU.mult, ALU.add))
                link(v.tensor_reduce(row_max[:], score[:].rearrange("p k h -> p h k"), AX_X, ALU.max))
                link(v.scalar_tensor_tensor(row_ref[:], row_max[:], 0.1 * NEG, row_max[:], ALU.is_gt, ALU.mult))
                assert n[0] == SC
                v.tensor_tensor(shifted[:, b, :].rearrange("p (k h) -> p k h", k=SLOTS), score[:],
                                row_ref[:].unsqueeze(1).to_broadcast([P, SLOTS, H]),
                                ALU.subtract).then_inc(s_shifted, 1)

            PR = 4

            def weigh(j, b):
                t = RING * j + b
                n = [0]

                def link(ins):
                    n[0] += 1
                    ins.then_inc(s_pr, 1)
                    dve.wait_ge(s_pr, PR * t + n[0])

                dve.wait_ge(s_exp, t + 1)
                e = expd[:, b, :].rearrange("p (k h) -> p k h", k=SLOTS)
                link(v.tensor_reduce(denom[:], e.rearrange("p k h -> p h k"), AX_X, ALU.add))
                link(v.tensor_single_scalar(denom1[:], denom[:], 0.5, ALU.max))
                link(v.reciprocal(rdenom[:], denom1[:]))
                link(v.tensor_tensor(prob[:], e, rdenom[:].unsqueeze(1).to_broadcast([P, SLOTS, H]), ALU.mult))
                assert n[0] == PR
                g = gathered[:, b, :].rearrange("p (k r) -> p k r", k=SLOTS)[:, :, 0:HF].rearrange(
                    "p k (h d) -> p k h d", h=H)
                v.tensor_tensor(g, g, prob[:].unsqueeze(3).to_broadcast([P, SLOTS, H, HD]),
                                ALU.mult).then_inc(s_weighted, 1)

            def finish(j, b, first):
                t = RING * j + b
                dve.wait_ge(s_reduced, t + 1)
                if not first:
                    dve.wait_ge(s_stored[b], 16 * j)
                v.tensor_tensor(out_tile[:, b, :], ps_out[:, b % 2, 0:HF],
                                base[:, bass.ds(t, 1), :].rearrange("p o d -> p (o d)"), ALU.add).then_inc(s_out, 1)

            def body(j, first, second):
                for b in range(RING):
                    prev = (j, b - 2) if b >= 2 else (j - 1, b + 2)
                    has_prev = b >= 2 or not first
                    if has_prev:
                        scores(*prev)
                    extract(j, b, first)
                    if has_prev:
                        weigh(*prev)
                    if b >= 3:
                        finish(j, b - 3, first)
                    elif not first:
                        finish(j - 1, b + 1, second)

            body(0, True, False)
            body(1, False, True)
            with dve.Fori(2, TILES // RING) as j:
                body(j, False, False)
            last = TILES // RING - 1
            for b in range(2, RING):
                scores(last, b)
                weigh(last, b)
                finish(last, b - 1, False)
            finish(last, RING - 1, False)

            v.tensor_reduce(missed[:, 0:1], adj_sum[:], AX_X, ALU.add).then_inc(s_check, 1)
            v.tensor_reduce(missed[:, 1:2], empty_sum[:], AX_X, ALU.add).then_inc(s_check, 1)
            dve.wait_ge(s_check, 2)
            v.scalar_tensor_tensor(missed[:, 2:3], missed[:, 1:2], 1.0 / EMPTY, missed[:, 0:1], ALU.mult,
                                   ALU.add).then_inc(s_check, 1)
            dve.wait_ge(s_check, 3)
            v.tensor_single_scalar(missed[:, 3:4], missed[:, 2:3], -float(SLOTS * TILES),
                                   ALU.add).then_inc(s_check, 1)
            dve.wait_ge(s_missed, 1)
            v.tensor_single_scalar(flag[:], ps_out[0:1, 0, 0:1], 0.0, ALU.not_equal).then_inc(s_flag, 1)
            dve.wait_ge(s_flag, 1)
            with dve.If(dve.value_load(flag[0:1, 0:1], min_val=0, max_val=1) > 0):
                LINKS = [8, 8]

                def dense_scores(i, c, second, link):
                    n = 2 * TILES * i + TILES * second + c
                    v.tensor_copy(dn_adjf, dn_adj[:, bass.ds(c * P, P)])
                    v.tensor_tensor(dn_diag, ident[:].unsqueeze(1).to_broadcast([P, H, P]),
                                    node[:, bass.ds(c, 1), 0:H].rearrange("p o h -> p h o").to_broadcast([P, H, P]),
                                    ALU.mult).then_inc(d_diag, 1)
                    dve.wait_ge(d_f1, n + 1)
                    link(v.tensor_tensor(dn_s, ps_f1, node[:, bass.ds(i, 1), H:].rearrange(
                        "p o h -> p h o").to_broadcast([P, H, P]), ALU.add))
                    link(v.scalar_tensor_tensor(dn_s, dn_s, SLOPE, dn_s, ALU.mult, ALU.max))
                    link(v.tensor_tensor(dn_s, dn_s, dn_adjf.unsqueeze(1).to_broadcast([P, H, P]), ALU.mult))
                    link(v.tensor_scalar(dn_zero, dn_s, 0.0, NEG, ALU.is_equal, ALU.mult))
                    link(v.tensor_tensor(dn_s, dn_s, dn_zero, ALU.add))

                def chain(at, second):
                    n = [0]

                    def link(ins):
                        n[0] += 1
                        ins.then_inc(d_chain[second], 1)
                        dve.wait_ge(d_chain[second], LINKS[second] * at + n[0])
                    return n, link

                with dve.Fori(0, TILES) as i:
                    v.memset(dn_acc, 0.0).then_inc(d_tail, 1)
                    v.memset(dn_den, 0.0).then_inc(d_tail, 1)
                    v.memset(dn_max, NEG).then_inc(d_tail, 1)
                    dve.wait_ge(d_tail, 6 * i + 3)
                    dve.sem_inc(d_init)
                    dve.sem_inc(d_acc)
                    dve.wait_ge(d_adj_in, 16 * (i + 1))
                    dve.sem_inc(s_gate_dve)
                    with dve.Fori(0, TILES) as c:
                        n, link = chain(TILES * i + c, 0)
                        dense_scores(i, c, 0, link)
                        link(v.tensor_reduce(dn_part, dn_s, AX_X, ALU.max))
                        link(v.tensor_tensor(dn_max, dn_max, dn_part, ALU.max))
                        link(v.scalar_tensor_tensor(dn_ref, dn_max, 0.1 * NEG, dn_max, ALU.is_gt, ALU.mult))
                        assert n[0] == LINKS[0]
                    with dve.Fori(0, TILES) as c:
                        at = TILES * i + c
                        n, link = chain(at, 1)
                        dense_scores(i, c, 1, link)
                        v.tensor_tensor(dn_s, dn_s, dn_ref.unsqueeze(2).to_broadcast([P, H, P]),
                                        ALU.subtract).then_inc(d_shift, 1)
                        dve.wait_ge(d_exp, at + 1)
                        link(v.tensor_reduce(dn_part, dn_e, AX_X, ALU.add))
                        link(v.tensor_tensor(dn_den, dn_den, dn_part, ALU.add))
                        dve.wait_ge(d_part, at + 1)
                        link(v.tensor_tensor(dn_acc, dn_acc, ps_out[:, 0, 0:HF], ALU.add))
                        assert n[0] == LINKS[1]
                        dve.sem_inc(d_acc)
                    v.tensor_single_scalar(dn_den, dn_den, 0.5, ALU.max).then_inc(d_tail, 1)
                    dve.wait_ge(d_tail, 6 * i + 4)
                    v.reciprocal(dn_rden, dn_den).then_inc(d_tail, 1)
                    dve.wait_ge(d_tail, 6 * i + 5)
                    v.tensor_tensor(dn_acc.rearrange("p (h d) -> p h d", h=H), dn_acc.rearrange("p (h d) -> p h d", h=H),
                                    dn_rden.unsqueeze(2).to_broadcast([P, H, HD]), ALU.mult).then_inc(d_tail, 1)
                    dve.wait_ge(d_tail, 6 * i + 6)
                    v.tensor_tensor(out_tile[:, 0, :], dn_acc,
                                    base[:, bass.ds(i, 1), :].rearrange("p o d -> p (o d)"), ALU.add).then_inc(d_out, 1)
                    dve.wait_ge(d_stored, 16 * (i + 1))


def kernel(x, adj, L0_gnn_weight, L0_gnn_weight_u, L0_gnn_weight_v, L0_gnn_bias, L0_gnn_proj_w, L0_gnn_proj_b):
    import numpy as _np
    import concourse.bacc as _bacc
    from concourse import mybir as _mybir
    from concourse.bass_utils import run_bass_kernel_spmd as _run

    nc = _bacc.Bacc("TRN2", target_bir_lowering=False, num_devices=1)
    given = {"x": x, "adj": adj, "weight": L0_gnn_weight, "weight_u": L0_gnn_weight_u,
             "weight_v": L0_gnn_weight_v, "bias": L0_gnn_bias,
             "proj_wT": _np.asarray(L0_gnn_proj_w).T, "proj_b": L0_gnn_proj_b}
    arrays, args = {}, []
    for name, a in given.items():
        a = _np.ascontiguousarray(a)
        arrays[f"in_{name}"] = a
        args.append(nc.dram_tensor(f"in_{name}", a.shape, _mybir.dt.from_np(a.dtype), kind="ExternalInput").ap())
    out = nc.dram_tensor("out", tuple(x.shape), F32, kind="ExternalOutput").ap()
    gat_kernel(nc, *args, out)
    r = _run(nc, [arrays], core_ids=[0])
    return r.results[0]["out"]
```

```python
from contextlib import ExitStack

import concourse.bass as bass
from concourse import mybir

ALU = mybir.AluOpType
ACT = mybir.ActivationFunctionType
F32 = mybir.dt.float32
F16 = mybir.dt.float16
BF16 = mybir.dt.bfloat16
I32 = mybir.dt.int32
U32 = mybir.dt.uint32
AX_X = mybir.AxisListType.X

P = 128
SLOTS = 16
CHUNKS = 5
EDGES = CHUNKS * P
BITS = 8
RING = 4
PICKS = 3
GROUP = 4
EMPTY = float(2 ** 20)
NEG = -1e30
SLOPE = 0.2
EPS = 1e-5


def gat_kernel(nc, x, adj, weight, weight_u, weight_v, bias, proj_wT, proj_b, out):
    N, D = x.shape
    H, HD = weight_u.shape[0], weight_u.shape[1]
    HF = H * HD
    KC = D // P
    TILES = N // P
    WORDS = N // BITS
    ROWS_STEP = P // BITS
    UNITS = 4
    UT = BITS // UNITS
    BANKS = WORDS // 512
    CANDS = 64
    SEG = WORDS // (CANDS // 8)
    ROW = HF + H
    STAGE = 2 * HF + 2 * H
    GROUPS = TILES // GROUP
    ROUNDS = TILES // RING
    assert GROUPS + PICKS * ROUNDS == TILES
    R_OFF, R_MID, R_ROW, R_F2 = SLOTS, SLOTS + 1, SLOTS + 2, SLOTS + 3
    REC = R_F2 + H

    with ExitStack() as ctx:
        def sb(name, shape, dt=F32):
            return ctx.enter_context(nc.sbuf_tensor(name, shape, dt))

        def ps(name, shape):
            return ctx.enter_context(nc.psum_tensor(name, shape, F32))

        def sem(name):
            return ctx.enter_context(nc.semaphore(name))

        table = nc.dram_tensor("support_table", (N, ROW), F32, kind="Internal").ap()

        adj_raw = sb("adj_raw", [P, UNITS, UT, WORDS], I32)
        adj_bf = sb("adj_bf", [P, UNITS, UT, WORDS], BF16)
        base = sb("base", [P, TILES, HF])
        node = sb("node", [P, TILES, 2 * H])
        record = sb("record", [P, TILES, REC])
        slot_pen = sb("slot_pen", [P, TILES, SLOTS])
        reach = sb("reach", [P, TILES])
        adj_sum = sb("adj_sum", [P, TILES * UNITS])
        out_tile = sb("out_tile", [P, RING, HF])
        EW = CHUNKS * ROW
        att = sb("att", [P, RING * (EW + 2 * EDGES)])
        gathered = att[:, 0:RING * EW].rearrange("p (b c r) -> p b c r", b=RING, c=CHUNKS)
        onehot = att[:, RING * EW:RING * (EW + EDGES)].rearrange("p (b e) -> p b e", b=RING)
        onehotT = att[:, RING * (EW + EDGES):].rearrange("p (b c r) -> p b c r", b=RING, c=CHUNKS)
        XN = 2 * GROUP * D
        x_in = att[:, 0:XN].rearrange("p (b i d) -> p b i d", b=2, i=GROUP)
        xhat = att[:, XN:2 * XN].rearrange("p (b i d) -> p b i d", b=2, i=GROUP)
        stage = att[:, 2 * XN:2 * XN + 2 * GROUP * STAGE].rearrange("p (b i d) -> p b i d", b=2, i=GROUP)
        uv_tmp = out_tile[:].rearrange("p (q c) d -> p q c d", q=2)
        ident = sb("ident", [P, P])
        ones_f = sb("ones_f", [P, P])
        before = sb("before", [P, P])
        minus_mid = sb("minus_mid", [P, P])
        w_all = sb("w_all", [P, KC, 2 * HF])
        w_uv = sb("w_uv", [P, KC, 2 * H])
        uv_row = sb("uv_row", [P, 2, HF])
        bias_row = sb("bias_row", [P, HF])
        projb_row = sb("projb_row", [P, HF])
        eps_col = sb("eps_col", [P, 1])
        pack_w = sb("pack_w", [P, BITS, P], BF16)
        pack_i = sb("pack_i", [P, 1], I32)
        pack_blk = sb("pack_blk", [P, ROWS_STEP])
        ones_row = sb("ones_row", [1, P], BF16)
        place_lo = sb("place_lo", [1, WORDS], BF16)
        place_hi = sb("place_hi", [1, WORDS], BF16)
        bit_shift = sb("bit_shift", [P, BITS], I32)
        bit_first = sb("bit_first", [P, BITS])
        edge_odd = sb("edge_odd", [P, EDGES])
        edge_at = sb("edge_at", [P, CHUNKS])
        slot_no = sb("slot_no", [P, SLOTS])
        row_no = sb("row_no", [P, P])
        hT = sb("hT", [P, 2, KC * P])
        stats = sb("stats", [P, GROUP, 6])
        mean_var = sb("mean_var", [P, GROUP, 2])
        std = sb("std", [P, GROUP])
        rstd = sb("rstd", [P, GROUP])
        cand = sb("cand", [P, CANDS])
        cand_rest = sb("cand_rest", [P, CANDS])
        words = sb("words", [P, SLOTS])
        words_i = sb("words_i", [P, SLOTS], I32)
        place_i = sb("place_i", [P, SLOTS], I32)
        bits = sb("bits", [P, SLOTS, BITS], I32)
        codes = sb("codes", [P, SLOTS, BITS])
        codes_rest = sb("codes_rest", [P, SLOTS * BITS])
        nbr = sb("nbr", [P, SLOTS])
        used = sb("used", [P, SLOTS])
        degree = sb("degree", [P, 1])
        distance = sb("distance", [P, EDGES])
        edge_rec = sb("edge_rec", [P, RING, CHUNKS, REC])
        edge_slot = sb("edge_slot", [P, CHUNKS])
        slot_hot = sb("slot_hot", [P, RING, CHUNKS, SLOTS])
        slot_nbr = sb("slot_nbr", [P, CHUNKS, SLOTS])
        edge_nbr = sb("edge_nbr", [P, CHUNKS])
        empty = sb("empty", [P, RING, CHUNKS])
        empty_sum = sb("empty_sum", [P, CHUNKS])
        idx = sb("idx", [P, RING, CHUNKS], U32)
        empty_pen = sb("empty_pen", [P, RING, CHUNKS])
        f2_edge = sb("f2_edge", [P, RING, CHUNKS, H])
        score = sb("score", [P, CHUNKS, H])
        zero_pen = sb("zero_pen", [P, CHUNKS, H])
        score_slot = sb("score_slot", [P, CHUNKS, SLOTS, H])
        row_score = sb("row_score", [P, SLOTS, H])
        row_max = sb("row_max", [P, H])
        row_ref = sb("row_ref", [P, H])
        shifted = sb("shifted", [P, CHUNKS, H])
        denom = sb("denom", [P, H])
        rdenom = sb("rdenom", [P, H])

        ps_words = ps("ps_words", [P, WORDS])
        ps_agg = ps("ps_agg", [P, 2, 512])
        ps_off = ps("ps_off", [P, 512])
        ps_rec = ps("ps_rec", [P, 512])
        ps_row = ps("ps_row", [P, 512])
        ps_ref = ps("ps_ref", [P, 512])
        ps_t = [ps_off, ps_rec]
        ps_f = [ps_row, ps_ref]

        s_w_in = sem("weights_in")
        s_uv = sem("weight_uv_ready")
        s_uv_mul = sem("weight_uv_products")
        s_pool_const = sem("pool_constants")
        s_dve_const = sem("dve_constants")
        s_pack_i = sem("pack_weights_value")
        s_gate_dve = sem("gate_dve")
        s_gate_pool = sem("gate_pool")
        s_x_in = [sem(f"x_in{b}") for b in range(2)]
        s_bn = sem("bn_stats_done")
        s_stats = sem("mean_var_ready")
        s_std = sem("std_ready")
        s_rstd = sem("rstd_ready")
        s_xhat = sem("xhat_ready")
        s_xT = sem("xT_ready")
        s_hT = sem("hT_ready")
        s_proj = sem("projected")
        s_staged = sem("staged")
        s_basev = sem("base_partial")
        s_based = sem("base_ready")
        s_rows_out = [sem(f"table_rows_out{b}") for b in range(2)]
        s_adj_in = [sem(f"adj_in{u}") for u in range(UNITS)]
        s_conv = sem("converted")
        s_adj_used = sem("adj_bf_used")
        s_words_read = sem("words_read")
        s_pick = sem("pick_chain")
        s_nbr = sem("neighbours_ready")
        s_degree = sem("degree_ready")
        s_recorded = sem("neighbours_recorded")
        s_offset = sem("offset_ready")
        s_filed = sem("offset_recorded")
        s_distance = sem("distance_ready")
        s_f2 = sem("f2_recorded")
        s_onehot = sem("onehot_ready")
        s_rec = sem("edge_records_ready")
        s_rec_sb = sem("edge_records_in_sbuf")
        s_pen = sem("empty_penalty_ready")
        s_f2e = sem("edge_f2_ready")
        s_ls = sem("list_chain")
        s_idx = sem("idx_ready")
        s_gather = [sem(f"rows_gathered{b}") for b in range(RING)]
        s_onehotT = sem("onehotT_ready")
        s_sc = sem("score_chain")
        s_score = sem("slot_scores_ready")
        s_row = sem("row_scores_ready")
        s_mx = sem("max_chain")
        s_ref = sem("row_ref_ready")
        s_refe = sem("edge_ref_ready")
        s_shifted = sem("shifted_ready")
        s_exp = sem("exp_ready")
        s_weighted = sem("weighted_ready")
        s_agg = sem("aggregated")
        s_nm = sem("normalise_chain")
        s_normed = sem("normalised")
        s_out = sem("out_ready")
        s_stored = [sem(f"out_stored{b}") for b in range(RING)]
        s_check = sem("check_chain")
        s_missed = sem("missed_summed")
        s_flag = sem("flag_ready")
        d_init = sem("dense_tile_ready")
        d_adj_in = sem("dense_adj_in")
        d_diag = sem("dense_f1_diagonal")
        d_f1 = sem("dense_f1_spread")
        d_chain = [sem("dense_max_chain"), sem("dense_sum_chain")]
        d_shift = sem("dense_shifted")
        d_exp = sem("dense_exp")
        d_expT = sem("dense_exp_transposed")
        d_expT_sb = sem("dense_exp_transposed_in_sbuf")
        d_sup_in = sem("dense_support_in")
        d_part = sem("dense_partial_product")
        d_acc = sem("dense_accumulated")
        d_tail = sem("dense_tail_chain")
        d_out = sem("dense_out_ready")
        d_stored = sem("dense_out_stored")


        missed = sb("missed", [P, 4])
        flag = sb("flag", [1, 1], I32)
        dn_adj = adj_raw[:].rearrange("p u s e -> p (u s e)")
        dn_adjf = att[:, 0:P]
        dn_diag, dn_s, dn_zero, dn_e, dn_eT = (
            att[:, P + q * H * P:P + (q + 1) * H * P].rearrange("p (h m) -> p h m", h=H) for q in range(5))
        dn_rest = att[:, P + 5 * H * P:]
        dn_acc = dn_rest[:, 0:HF]
        dn_sup = dn_rest[:, HF:2 * HF]
        dn_max, dn_part, dn_ref, dn_den, dn_rden = (
            dn_rest[:, 2 * HF + q * H:2 * HF + (q + 1) * H] for q in range(5))
        ps_f1 = ps_words[:, 0:H * P].rearrange("p (h m) -> p h m", h=H)
        ps_eT = ps_words[:, 512:512 + H * P].rearrange("p (h m) -> p h m", h=H)

        adj_v = adj.rearrange("(T u s n) (m e) -> T u (n m) s e", u=UNITS, s=UT, n=ROWS_STEP, m=BITS)
        x_v = x.rearrange("(g i p) d -> g p i d", i=GROUP, p=P)
        table_v = table.rearrange("(g i p) d -> g p i d", i=GROUP, p=P)
        out_v = out.rearrange("(t p) d -> t p d", p=P)
        adj_rows = adj.rearrange("(t p) m -> t p m", p=P)
        table_rows = table[:, 0:HF].rearrange("(t p) d -> t p d", p=P)

        def lagged(i, b, lag):
            back = -((b - lag) // RING)
            return i - back, b - lag + back * RING

        block = ctx.enter_context(nc.Block())

        @block.sync
        def _(sp):
            def load_x(j, b, first):
                g = 2 * j + b
                if not first:
                    sp.wait_ge(s_xhat, GROUP * (g - 1))
                    sp.wait_ge(s_based, GROUP * (g - 1))
                sp.dma_start(x_in[:, b], x_v[g]).then_inc(s_x_in[b], 16)

            def load_adj(t, first=False):
                for u in range(UNITS):
                    if not first:
                        sp.wait_ge(s_conv, UNITS * (t - 1) + u + 1)
                    sp.dma_start(adj_raw[:, u], adj_v[t, u]).then_inc(s_adj_in[u], 16)

            def store_out(i, b):
                sp.wait_ge(s_out, RING * i + b + 1)
                sp.dma_start(out_v[RING * i + b], out_tile[:, b, :]).then_inc(s_stored[b], 16)

            load_x(0, 0, True)
            for dst, src in ((uv_row[:, 0, :], weight_u.rearrange("h d o -> o (h d)")),
                             (uv_row[:, 1, :], weight_v.rearrange("h d o -> o (h d)")),
                             (bias_row[:, :], bias),
                             (projb_row[:, :], proj_b.rearrange("(o d) -> o d", o=1))):
                sp.dma_start(dst, src.to_broadcast([P, HF])).then_inc(s_w_in, 16)
            for c in range(KC):
                sp.dma_start(w_all[:, c, 0:HF], proj_wT[c * P:(c + 1) * P, :]).then_inc(s_w_in, 16)
                sp.dma_start(w_all[:, c, HF:], weight[c * P:(c + 1) * P, :]).then_inc(s_w_in, 16)
            load_adj(0, True)
            load_x(0, 1, True)
            load_adj(1)
            with sp.Fori(1, GROUPS // 2) as j:
                for b in range(2):
                    load_adj(2 * j + b)
                    load_x(j, b, False)
            for b in range(RING):
                sp.sem_inc(s_stored[b], 16)

            def attend(i, first, second):
                for b in range(RING):
                    if b < PICKS:
                        load_adj(GROUPS + PICKS * i + b)
                    if not first and not (second and b < 2):
                        store_out(*lagged(i, b, 6))

            attend(0, True, False)
            attend(1, False, True)
            with sp.Fori(2, ROUNDS) as i:
                attend(i, False, False)
            for b in range(2, RING):
                store_out(ROUNDS - 2, b)
            for b in range(RING):
                store_out(ROUNDS - 1, b)
            for b in range(RING):
                sp.wait_ge(s_stored[b], 16 * (ROUNDS + 1))

            sp.wait_ge(s_flag, 1)
            with sp.If(sp.value_load(flag[0:1, 0:1], min_val=0, max_val=1) > 0):
                with sp.Fori(0, TILES) as i:
                    sp.wait_ge(d_init, i + 1)
                    sp.dma_start(dn_adj, adj_rows[i]).then_inc(d_adj_in, 16)
                    with sp.Fori(0, TILES) as c:
                        sp.wait_ge(d_acc, TILES * i + c + i + 1)
                        sp.dma_start(dn_sup, table_rows[c]).then_inc(d_sup_in, 16)
                    sp.wait_ge(d_out, i + 1)
                    sp.dma_start(out_v[i], out_tile[:, 0, :]).then_inc(d_stored, 16)
                sp.wait_ge(d_stored, 16 * TILES)

        @block.tensor
        def _(pe):
            def transposes(t, b, first):
                pe.wait_ge(s_xhat, t + 1)
                if not first:
                    pe.wait_ge(s_hT, t - 1)
                for c in range(KC):
                    mm = nc.tensor.transpose(ps_t[b % 2][:, c * P:(c + 1) * P],
                                             xhat[:, b // GROUP, b % GROUP, c * P:(c + 1) * P], ident[:])
                mm.then_inc(s_xT, 1)

            def project(t, b, first):
                pe.wait_ge(s_hT, t + 1)
                if not first:
                    pe.wait_ge(s_staged, t - 1)
                for c in range(KC):
                    nc.tensor.matmul(ps_agg[:, b % 2, :], hT[:, b % 2, c * P:(c + 1) * P], w_all[:, c, :],
                                     start=(c == 0), stop=(c == KC - 1))
                for c in range(KC):
                    mm = nc.tensor.matmul(ps_f[b % 2][:, 0:2 * H], hT[:, b % 2, c * P:(c + 1) * P],
                                          w_uv[:, c, :], start=(c == 0), stop=(c == KC - 1))
                mm.then_inc(s_proj, 1)

            def pack(t, first=False):
                if not first:
                    pe.wait_ge(s_words_read, t)
                for k in range(BANKS):
                    for row in (place_lo, place_hi):
                        nc.tensor.matmul(ps_words[:, k * 512:(k + 1) * 512], ones_row[:],
                                         row[:, k * 512:(k + 1) * 512], start=(row is place_lo), stop=False)
                for u in range(UNITS):
                    pe.wait_ge(s_conv, UNITS * t + u + 1)
                    for s in range(UT):
                        for k in range(BANKS):
                            mm = nc.tensor.matmul(ps_words[:, k * 512:(k + 1) * 512], pack_w[:, u * UT + s, :],
                                                  adj_bf[:, u, s, k * 512:(k + 1) * 512],
                                                  start=False, stop=(u == UNITS - 1 and s == UT - 1))
                    mm.then_inc(s_adj_used, 1)

            pe.wait_ge(s_pool_const, 7)
            pe.wait_ge(s_dve_const, 8)
            pack(0, True)
            pe.wait_ge(s_w_in, 16 * (2 * KC + 4))
            pe.wait_ge(s_uv, 4)

            def offsets(t, o):
                pe.wait_ge(s_degree, t + 1)
                nc.tensor.matmul(o[:, 0:1], before[:], degree[:], start=True, stop=True)
                nc.tensor.matmul(o[:, 1:2], minus_mid[:], degree[:], start=True, stop=True).then_inc(s_offset, 1)

            def tables(j, first):
                for gb in range(2):
                    for q in range(GROUP + 1):
                        b = gb * GROUP + q
                        if q < GROUP:
                            transposes(2 * GROUP * j + b, b, first and b < 2)
                        if q > 0:
                            project(2 * GROUP * j + b - 1, b - 1, first and b - 1 < 2)
                    pack(2 * j + gb + 1)
                    pe.wait_ge(s_staged, GROUP * (2 * j + gb + 1))
                    offsets(2 * j + gb, ps_f[1][:, 2 * H:])

            tables(0, True)
            with pe.Fori(1, GROUPS // 2) as j:
                tables(j, False)

            def edge_records(i, b):
                pe.wait_ge(s_onehot, RING * i + b + 1)
                for c in range(CHUNKS):
                    mm = nc.tensor.matmul(ps_rec[:, c * REC:(c + 1) * REC], onehot[:, b, c * P:(c + 1) * P],
                                          record[:, bass.ds(RING * i + b, 1), :].rearrange("p o r -> p (o r)"),
                                          start=True, stop=True)
                mm.then_inc(s_rec, 1)

            def row_scores(i, b):
                pe.wait_ge(s_onehotT, RING * i + b + 1)
                pe.wait_ge(s_score, RING * i + b + 1)
                for c in range(CHUNKS):
                    mm = nc.tensor.matmul(ps_row[:, 0:SLOTS * H], onehotT[:, b, c, :],
                                          score_slot[:, c].rearrange("p k h -> p (k h)"),
                                          start=(c == 0), stop=(c == CHUNKS - 1))
                mm.then_inc(s_row, 1)

            def edge_refs(i, b):
                pe.wait_ge(s_ref, RING * i + b + 1)
                for c in range(CHUNKS):
                    mm = nc.tensor.matmul(ps_ref[:, c * H:(c + 1) * H], onehot[:, b, c * P:(c + 1) * P],
                                          row_ref[:], start=True, stop=True)
                mm.then_inc(s_refe, 1)

            def aggregate(i, b):
                pe.wait_ge(s_weighted, RING * i + b + 1)
                for c in range(CHUNKS):
                    mm = nc.tensor.matmul(ps_agg[:, b % 2, 0:ROW], onehotT[:, b, c, :], gathered[:, b, c, :],
                                          start=(c == 0), stop=(c == CHUNKS - 1))
                mm.then_inc(s_agg, 1)

            pe.wait_ge(s_staged, TILES)

            def attend(i, first, last):
                for b in range(RING):
                    behind, two = lagged(i, b, 2), b >= 2 or not first
                    if b >= 3 or not first:
                        aggregate(*lagged(i, b, 3))
                    edge_records(i, b)
                    if two:
                        row_scores(*behind)
                        edge_refs(*behind)
                    if last and b < PICKS:
                        offsets(GROUPS + PICKS * i + b, ps_off)
                    if b < PICKS and not (last and b == PICKS - 1):
                        pack(GROUPS + PICKS * i + b + 1)
                    if not last and b < PICKS:
                        offsets(GROUPS + PICKS * i + b, ps_off)

            attend(0, True, False)
            with pe.Fori(1, ROUNDS - 1) as i:
                attend(i, False, False)
            attend(ROUNDS - 1, False, True)
            for b in range(2, RING):
                aggregate(ROUNDS - 1, b - 1)
                row_scores(ROUNDS - 1, b)
                edge_refs(ROUNDS - 1, b)
            aggregate(ROUNDS - 1, RING - 1)

            pe.wait_ge(s_check, 4)
            nc.tensor.matmul(ps_agg[0:1, 0, 0:1], missed[:, 3:4], ones_f[:, 0:1], start=True,
                             stop=True).then_inc(s_missed, 1)
            pe.wait_ge(s_flag, 1)
            with pe.If(pe.value_load(flag[0:1, 0:1], min_val=0, max_val=1) > 0):
                def spread_f1(n):
                    pe.wait_ge(d_diag, n + 1)
                    nc.tensor.matmul(ps_f1, ones_f[:], dn_diag, start=True, stop=True).then_inc(d_f1, 1)

                with pe.Fori(0, TILES) as i:
                    with pe.Fori(0, TILES) as c:
                        spread_f1(2 * TILES * i + c)
                    with pe.Fori(0, TILES) as c:
                        spread_f1(2 * TILES * i + TILES + c)
                        pe.wait_ge(d_exp, TILES * i + c + 1)
                        for h in range(H):
                            mm = nc.tensor.transpose(ps_eT[:, h, :], dn_e[:, h, :], ident[:])
                        mm.then_inc(d_expT, 1)
                        pe.wait_ge(d_sup_in, 16 * (TILES * i + c + 1))
                        pe.wait_ge(d_expT_sb, TILES * i + c + 1)
                        for h in range(H):
                            mm = nc.tensor.matmul(ps_agg[:, 0, h * HD:(h + 1) * HD], dn_eT[:, h, :],
                                                  dn_sup[:, h * HD:(h + 1) * HD], start=True, stop=True)
                        mm.then_inc(d_part, 1)

        @block.scalar
        def _(act):
            def convert(t, units, first=False):
                for u in units:
                    act.wait_ge(s_adj_in[u], 16 * (t + 1))
                    if not first:
                        act.wait_ge(s_adj_used, UNITS * (t - 1) + u + 1)
                    nc.scalar.activation(adj_bf[:, u], adj_raw[:, u], ACT.Copy,
                                         accum_out=adj_sum[:, bass.ds(UNITS * t + u, 1)]).then_inc(s_conv, 1)

            def record_nbrs(t):
                act.wait_ge(s_nbr, t + 1)
                nc.scalar.activation(record[:, bass.ds(t, 1), 0:SLOTS].rearrange("p o k -> p (o k)"), nbr[:], ACT.Copy)
                nc.scalar.activation(used[:], nbr[:], ACT.Sign, accum_out=degree[:]).then_inc(s_degree, 1)
                act.wait_ge(s_degree, t + 1)
                nc.scalar.activation(slot_pen[:, bass.ds(t, 1), :].rearrange("p o k -> p (o k)"), used[:], ACT.Copy,
                                     scale=-NEG, bias=NEG)
                nc.scalar.activation(reach[:, bass.ds(t, 1)], degree[:], ACT.Square, scale=0.5).then_inc(s_recorded, 1)

            def record_offset(t, o):
                act.wait_ge(s_offset, t + 1)
                nc.scalar.activation(record[:, bass.ds(t, 1), R_OFF:R_MID + 1].rearrange("p o k -> p (o k)"),
                                     o[:, 0:2], ACT.Copy).then_inc(s_filed, 1)

            def deviation(g):
                act.wait_ge(s_stats, g + 1)
                nc.scalar.activation(std[:], mean_var[:, :, 1], ACT.Sqrt, bias=eps_col[:, 0:1]).then_inc(s_std, 1)

            def tables(j, first, last):
                for gb in range(2):
                    g = 2 * j + gb
                    if not first:
                        act.wait_ge(s_based, GROUP * (g - 1))
                        act.wait_ge(s_rows_out[gb], 16 * j)
                    for q in range(GROUP + 1):
                        b = gb * GROUP + q
                        t = 2 * GROUP * j + b
                        if q < GROUP:
                            act.wait_ge(s_xT, t + 1)
                            if not (first and b < 2):
                                act.wait_ge(s_proj, t - 1)
                            nc.scalar.activation(hT[:, b % 2, :], ps_t[b % 2][:, 0:KC * P],
                                                 ACT.Relu).then_inc(s_hT, 1)
                        if q == 0 and not (first and gb == 0):
                            record_offset(g - 1, ps_f[1][:, 2 * H:])
                        if q > 0:
                            act.wait_ge(s_proj, t)
                            nc.scalar.activation(stage[:, gb, q - 1, 0:2 * HF], ps_agg[:, (b - 1) % 2, :],
                                                 ACT.Copy)
                            nc.scalar.activation(stage[:, gb, q - 1, 2 * HF:STAGE], ps_f[(b - 1) % 2][:, 0:2 * H],
                                                 ACT.Copy).then_inc(s_staged, 1)
                        if q < GROUP:
                            convert(g + 1, [q])
                        if q == 2 and not (last and gb == 1):
                            deviation(g + 1)
                    record_nbrs(g)
                    act.wait_ge(s_staged, GROUP * (g + 1))
                    act.dma_start(table_v[g], stage[:, gb, :, HF:HF + ROW]).then_inc(s_rows_out[gb], 16)

            act.wait_ge(s_dve_const, 8)
            convert(0, range(UNITS), True)
            deviation(0)
            tables(0, True, False)
            with act.Fori(1, GROUPS // 2 - 1) as j:
                tables(j, False, False)
            tables(GROUPS // 2 - 1, False, True)

            def exponential(i, b):
                act.wait_ge(s_shifted, RING * i + b + 1)
                nc.scalar.activation(gathered[:, b, :, HF:], shifted[:], ACT.Exp).then_inc(s_exp, 1)

            def distances(i, b, first=False):
                t = RING * i + b
                act.wait_ge(s_filed, t + 1)
                if not first:
                    act.wait_ge(s_onehot, t)
                nc.scalar.activation(distance[:], edge_odd[:], ACT.Square, scale=0.5,
                                     bias=record[:, bass.ds(t, 1), R_MID:R_MID + 1].rearrange(
                                         "p o k -> p (o k)")).then_inc(s_distance, 1)

            def record_edges(i, b):
                act.wait_ge(s_rec, RING * i + b + 1)
                nc.scalar.activation(edge_rec[:, b].rearrange("p c r -> p (c r)"), ps_rec[:, 0:CHUNKS * REC],
                                     ACT.Copy).then_inc(s_rec_sb, 1)

            def attend(i, first, last):
                for b in range(RING):
                    picks = b < PICKS and not (last and b == PICKS - 1)
                    t = GROUPS + PICKS * i + b
                    if picks:
                        convert(t + 1, range(0, 1))
                    record_edges(i, b)
                    if picks:
                        convert(t + 1, range(1, 3))
                    if b < PICKS:
                        record_nbrs(t)
                    if b >= 2 or not first:
                        exponential(*lagged(i, b, 2))
                    if last and b < PICKS:
                        record_offset(t, ps_off)
                    if not (last and b == RING - 1):
                        distances(*((i, b + 1) if b < RING - 1 else (i + 1, 0)))
                    if picks:
                        convert(t + 1, range(3, UNITS))
                    if not last and b < PICKS:
                        record_offset(t, ps_off)

            record_offset(GROUPS - 1, ps_f[1][:, 2 * H:])
            distances(0, 0, True)
            attend(0, True, False)
            with act.Fori(1, ROUNDS - 1) as i:
                attend(i, False, False)
            attend(ROUNDS - 1, False, True)
            for b in range(2, RING):
                exponential(ROUNDS - 1, b)

            act.wait_ge(s_flag, 1)
            with act.If(act.value_load(flag[0:1, 0:1], min_val=0, max_val=1) > 0):
                with act.Fori(0, TILES * TILES) as n:
                    act.wait_ge(d_shift, n + 1)
                    nc.scalar.activation(dn_e, dn_s, ACT.Exp).then_inc(d_exp, 1)
                    act.wait_ge(d_expT, n + 1)
                    nc.scalar.activation(dn_eT, ps_eT, ACT.Copy).then_inc(d_expT_sb, 1)

        @block.gpsimd
        def _(pool):
            ramp = dict(allow_small_or_imprecise_dtypes=True)
            pool.memset(ident[:], 0.0).then_inc(s_pool_const, 1)
            pool.memset(pack_blk[:], 1.0).then_inc(s_pool_const, 1)
            pool.iota(pack_i[:], [[0, 1]], base=0, channel_multiplier=1).then_inc(s_pool_const, 1)
            pool.iota(place_lo[:], [[0, WORDS // 256], [1, 256]], base=0, channel_multiplier=0,
                      **ramp).then_inc(s_pool_const, 1)
            pool.iota(place_hi[:], [[256, WORDS // 256], [0, 256]], base=0, channel_multiplier=0,
                      **ramp).then_inc(s_pool_const, 1)
            pool.wait_ge(s_pool_const, 5)
            pool.affine_select(pack_blk[:], pack_blk[:], [[-BITS, ROWS_STEP]], ALU.is_ge, 0.0, base=0,
                               channel_multiplier=1).then_inc(s_pool_const, 1)
            pool.wait_ge(s_pool_const, 6)
            pool.affine_select(pack_blk[:], pack_blk[:], [[BITS, ROWS_STEP]], ALU.is_ge, 0.0, base=BITS - 1,
                               channel_multiplier=-1).then_inc(s_pool_const, 1)
            pool.iota(bit_shift[:], [[1, BITS]], base=WORDS.bit_length() - 1,
                      channel_multiplier=0).then_inc(s_pool_const, 1)
            pool.iota(bit_first[:], [[WORDS, BITS]], base=1, channel_multiplier=0, **ramp).then_inc(s_pool_const, 1)
            pool.affine_select(ident[:], ident[:], [[-1, P]], ALU.not_equal, 1.0, base=0,
                               channel_multiplier=1).then_inc(s_pool_const, 1)
            pool.memset(before[:], 1.0).then_inc(s_pool_const, 1)
            pool.wait_ge(s_pool_const, 11)
            pool.affine_select(before[:], before[:], [[1, P]], ALU.is_gt, 0.0, base=0,
                               channel_multiplier=-1).then_inc(s_pool_const, 1)
            pool.iota(edge_odd[:], [[2, EDGES]], base=1, channel_multiplier=0, **ramp).then_inc(s_pool_const, 1)
            pool.iota(edge_at[:], [[P, CHUNKS]], base=0, channel_multiplier=1, **ramp).then_inc(s_pool_const, 1)
            pool.iota(slot_no[:], [[1, SLOTS]], base=0, channel_multiplier=0, **ramp).then_inc(s_pool_const, 1)
            pool.iota(row_no[:], [[1, P]], base=1, channel_multiplier=0, **ramp).then_inc(s_pool_const, 1)
            pool.iota(record[:, :, R_ROW], [[0, TILES]], base=1, channel_multiplier=1,
                      **ramp).then_inc(s_pool_const, 1)
            pool.wait_ge(s_w_in, 16 * (2 * KC + 4))
            pool.tensor_tensor(bias_row[:], bias_row[:], projb_row[:], ALU.add).then_inc(s_pool_const, 1)
            pool.wait_ge(s_pool_const, 18)

            def tables(j):
                for gb in range(2):
                    pool.wait_ge(s_x_in[gb], 16 * (j + 1))
                    for q in range(GROUP):
                        t = GROUP * (2 * j + gb) + q
                        bt = base[:, bass.ds(t, 1), :].rearrange("p o d -> p (o d)")
                        pool.tensor_tensor(bt, x_in[:, gb, q, :], bias_row[:], ALU.add).then_inc(s_basev, 1)
                        pool.wait_ge(s_staged, t + 1)
                        pool.wait_ge(s_basev, t + 1)
                        pool.tensor_copy(node[:, bass.ds(t, 1), :].rearrange("p o d -> p (o d)"),
                                         stage[:, gb, q, 2 * HF:STAGE])
                        pool.tensor_copy(record[:, bass.ds(t, 1), R_F2:].rearrange("p o d -> p (o d)"),
                                         stage[:, gb, q, 2 * HF + H:STAGE])
                        pool.tensor_tensor(bt, bt, stage[:, gb, q, 0:HF], ALU.add).then_inc(s_based, 1)

            with pool.Fori(0, GROUPS // 2) as j:
                tables(j)

            for b in range(2):
                pool.wait_ge(s_rows_out[b], 16 * (GROUPS // 2))
            pool.wait_ge(s_xhat, TILES)
            pool.wait_ge(s_xT, TILES)
            pool.memset(att[:, 0:RING * EW], 0.0).then_inc(s_pool_const, 1)
            pool.wait_ge(s_pool_const, 19)

            def gather(i, b, first):
                t = RING * i + b
                pool.wait_ge(s_idx, t + 1)
                if not first:
                    pool.wait_ge(s_agg, t - RING + 1)
                pool.sem_inc(s_gate_pool)
                for c in range(CHUNKS):
                    pool.indirect_dma_start(gathered[:, b, c, :], None, table,
                                            bass.IndirectOffsetOnAxis(idx[:, b, c:c + 1], 0),
                                            bounds_check=N - 1, oob_is_err=False).then_inc(s_gather[b], 16)
                pool.tensor_scalar(empty_pen[:, b, :], edge_rec[:, b, :, R_ROW], 0.0, NEG, ALU.is_equal,
                                   ALU.mult).then_inc(s_pen, 1)
                for c in range(CHUNKS):
                    last = pool.tensor_scalar(onehotT[:, b, c, :], row_no[:], edge_rec[:, b, c, R_ROW:R_ROW + 1],
                                              None, ALU.is_equal)
                last.then_inc(s_onehotT, 1)
                pool.wait_ge(s_pen, t + 1)
                pool.tensor_tensor(f2_edge[:, b], empty_pen[:, b, :].unsqueeze(2).to_broadcast([P, CHUNKS, H]),
                                   edge_rec[:, b, :, R_F2:], ALU.add).then_inc(s_f2e, 1)

            def add_base(i, b):
                t = RING * i + b
                pool.wait_ge(s_normed, t + 1)
                pool.tensor_tensor(out_tile[:, b, :], out_tile[:, b, :],
                                   base[:, bass.ds(t, 1), :].rearrange("p o d -> p (o d)"), ALU.add).then_inc(s_out, 1)

            def attend(i, first):
                for b in range(RING):
                    gather(i, b, first)
                    if b >= 3 or not first:
                        add_base(*lagged(i, b, 3))

            attend(0, True)
            with pool.Fori(1, ROUNDS) as i:
                attend(i, False)
            for b in range(1, RING):
                add_base(ROUNDS - 1, b)

        @block.vector
        def _(dve):
            v = nc.vector

            def chain(sem_, at, links):
                n = [0]

                def link(ins):
                    n[0] += 1
                    assert n[0] <= links
                    ins.then_inc(sem_, 1)
                    dve.wait_ge(sem_, links * at + n[0])
                return link

            v.memset(eps_col[:], EPS).then_inc(s_dve_const, 1)
            v.memset(ones_f[:], 1.0).then_inc(s_dve_const, 1)
            v.memset(ones_row[:], 1.0).then_inc(s_dve_const, 1)
            v.memset(empty_sum[:], 0.0).then_inc(s_dve_const, 1)
            v.memset(pack_w[:], 0.0).then_inc(s_dve_const, 1)
            dve.wait_ge(s_pool_const, 7)
            v.tensor_single_scalar(pack_i[:], pack_i[:], BITS - 1, ALU.bitwise_and).then_inc(s_dve_const, 1)
            dve.wait_ge(s_dve_const, 6)
            v.tensor_single_scalar(pack_i[:], pack_i[:], 127 + WORDS.bit_length() - 1, ALU.add).then_inc(s_dve_const, 1)
            dve.wait_ge(s_dve_const, 7)
            v.tensor_single_scalar(pack_i[:], pack_i[:], 23, ALU.logical_shift_left).then_inc(s_pack_i, 1)
            dve.wait_ge(s_pack_i, 1)
            for s in range(BITS):
                last = v.tensor_scalar(pack_w[:, s, s * ROWS_STEP:(s + 1) * ROWS_STEP], pack_blk[:],
                                       pack_i[:].bitcast(F32)[:, 0:1], None, ALU.mult)
            dve.wait_ge(s_pool_const, 12)
            v.scalar_tensor_tensor(minus_mid[:], ident[:], -0.5, before[:], ALU.mult,
                                   ALU.subtract).then_inc(s_dve_const, 1)
            dve.wait_ge(s_w_in, 16 * (2 * KC + 4))
            for q in range(2):
                for c in range(KC):
                    v.tensor_tensor(uv_tmp[:, q, c], w_all[:, c, HF:], uv_row[:, q, :], ALU.mult).then_inc(s_uv_mul, 1)
            dve.wait_ge(s_uv_mul, 2 * KC)
            for q in range(2):
                for c in range(KC):
                    v.tensor_reduce(w_uv[:, c, q * H:(q + 1) * H],
                                    uv_tmp[:, q, c].rearrange("p (h d) -> p h d", h=H), AX_X,
                                    ALU.add).then_inc(s_uv, 1)

            PICK = 9

            def pick_words(t, link):
                dve.wait_ge(s_adj_used, UNITS * (t + 1))
                dve.sem_inc(s_gate_dve)
                for s in range(CANDS // 8):
                    last = v.max(cand[:, s * 8:(s + 1) * 8], ps_words[:, s * SEG:(s + 1) * SEG])
                last.then_inc(s_words_read, 1)
                dve.wait_ge(s_words_read, t + 1)
                dve.sem_inc(s_gate_dve)
                link(v.max(words[:, 0:8], cand[:]))
                dve.sem_inc(s_gate_dve)
                link(v.match_replace(cand_rest[:], words[:, 0:8], cand[:], 0.0))
                dve.sem_inc(s_gate_dve)
                link(v.max(words[:, 8:16], cand_rest[:]))

            def split_words(t, link, first=False):
                link(v.tensor_copy(words_i[:], words[:]))
                v.tensor_tensor(bits[:], words_i[:].unsqueeze(2).to_broadcast([P, SLOTS, BITS]),
                                bit_shift[:].unsqueeze(1).to_broadcast([P, SLOTS, BITS]), ALU.logical_shift_right)
                link(v.tensor_single_scalar(place_i[:], words_i[:], WORDS - 1, ALU.bitwise_and))
                v.tensor_tensor(codes[:], place_i[:].unsqueeze(2).to_broadcast([P, SLOTS, BITS]),
                                bit_first[:].unsqueeze(1).to_broadcast([P, SLOTS, BITS]), ALU.add)
                link(v.tensor_single_scalar(bits[:], bits[:], 1, ALU.bitwise_and))
                link(v.tensor_tensor(codes[:], codes[:], bits[:], ALU.mult))
                codes_f = codes[:].rearrange("p k b -> p (k b)")
                if not first:
                    dve.wait_ge(s_recorded, t)
                dve.sem_inc(s_gate_dve)
                link(v.max(nbr[:, 0:8], codes_f))
                dve.sem_inc(s_gate_dve)
                link(v.match_replace(codes_rest[:], nbr[:, 0:8], codes_f, 0.0))
                dve.sem_inc(s_gate_dve)
                v.max(nbr[:, 8:16], codes_rest[:]).then_inc(s_nbr, 1)

            dve.wait_ge(s_pool_const, 18)

            def tables(j, first):
                for gb in range(2):
                    g = 2 * j + gb
                    link = chain(s_pick, g, PICK)
                    dve.wait_ge(s_x_in[gb], 16 * (j + 1))
                    for q in range(GROUP):
                        last = v.bn_stats(stats[:, q, :], x_in[:, gb, q, :])
                    last.then_inc(s_bn, 1)
                    dve.wait_ge(s_bn, g + 1)
                    dve.sem_inc(s_gate_dve)
                    for q in range(GROUP):
                        last = v.bn_aggr(mean_var[:, q, :], stats[:, q, :])
                    last.then_inc(s_stats, 1)
                    dve.wait_ge(s_stats, g + 1)
                    dve.wait_ge(s_std, g + 1)
                    v.reciprocal(rstd[:], std[:]).then_inc(s_rstd, 1)
                    dve.wait_ge(s_rstd, g + 1)
                    if not first:
                        dve.wait_ge(s_xT, GROUP * (g - 1))
                    for q in range(GROUP):
                        v.tensor_scalar(xhat[:, gb, q, :], x_in[:, gb, q, :], mean_var[:, q, 0:1],
                                        rstd[:, q:q + 1], ALU.subtract, ALU.mult).then_inc(s_xhat, 1)
                    pick_words(g, link)
                    split_words(g, link, first and gb == 0)

            tables(0, True)
            with dve.Fori(1, GROUPS // 2) as j:
                tables(j, False)
            dve.wait_ge(s_based, TILES)
            for b in range(2):
                dve.wait_ge(s_rows_out[b], 16 * (GROUPS // 2))

            LS, SC, MX, NM = 4, 4, 2, 2

            def one_hot(i, b):
                t = RING * i + b
                dve.wait_ge(s_distance, t + 1)
                v.tensor_scalar(onehot[:, b, :], distance[:], reach[:, bass.ds(t, 1)], None,
                                ALU.is_lt).then_inc(s_onehot, 1)

            def edge_list(i, b):
                t = RING * i + b
                link = chain(s_ls, t, LS)
                dve.wait_ge(s_rec_sb, t + 1)
                v.tensor_scalar(empty[:, b, :], edge_rec[:, b, :, R_ROW], 0.0, EMPTY, ALU.is_equal, ALU.mult)
                link(v.tensor_tensor(edge_slot[:], edge_at[:], edge_rec[:, b, :, R_OFF], ALU.subtract))
                v.tensor_tensor(empty_sum[:], empty_sum[:], empty[:, b, :], ALU.add)
                link(v.tensor_tensor(slot_hot[:, b], slot_no[:].unsqueeze(1).to_broadcast([P, CHUNKS, SLOTS]),
                                     edge_slot[:].unsqueeze(2).to_broadcast([P, CHUNKS, SLOTS]), ALU.is_equal))
                link(v.tensor_tensor(slot_nbr[:], slot_hot[:, b], edge_rec[:, b, :, 0:SLOTS], ALU.mult))
                link(v.tensor_reduce(edge_nbr[:], slot_nbr[:], AX_X, ALU.add))
                v.scalar_tensor_tensor(idx[:, b, :], edge_nbr[:], -1.0, empty[:, b, :], ALU.add,
                                       ALU.add).then_inc(s_idx, 1)

            def scores(i, b):
                t = RING * i + b
                link = chain(s_sc, t, SC)
                dve.wait_ge(s_gather[b], 16 * CHUNKS * (i + 1))
                dve.wait_ge(s_f2e, t + 1)
                link(v.tensor_tensor(score[:], gathered[:, b, :, HF:], f2_edge[:, b], ALU.add))
                link(v.scalar_tensor_tensor(score[:], score[:], SLOPE, score[:], ALU.mult, ALU.max))
                link(v.tensor_scalar(zero_pen[:], score[:], 0.0, NEG, ALU.is_equal, ALU.mult))
                link(v.tensor_tensor(score[:], score[:], zero_pen[:], ALU.add))
                v.tensor_tensor(score_slot[:], slot_hot[:, b].unsqueeze(3).to_broadcast([P, CHUNKS, SLOTS, H]),
                                score[:].unsqueeze(2).to_broadcast([P, CHUNKS, SLOTS, H]),
                                ALU.mult).then_inc(s_score, 1)

            def row_maximum(i, b):
                t = RING * i + b
                link = chain(s_mx, t, MX)
                dve.wait_ge(s_row, t + 1)
                link(v.tensor_tensor(row_score[:], ps_row[:, 0:SLOTS * H].rearrange("p (k h) -> p k h", k=SLOTS),
                                     slot_pen[:, bass.ds(t, 1), :].rearrange("p o k -> p k o").to_broadcast([P, SLOTS, H]), ALU.add))
                link(v.tensor_reduce(row_max[:], row_score[:].rearrange("p k h -> p h k"), AX_X, ALU.max))
                v.scalar_tensor_tensor(row_ref[:], row_max[:], 0.1 * NEG, row_max[:], ALU.is_gt,
                                       ALU.mult).then_inc(s_ref, 1)

            def shift(i, b):
                dve.wait_ge(s_refe, RING * i + b + 1)
                v.tensor_tensor(shifted[:], score[:], ps_ref[:, 0:CHUNKS * H].rearrange("p (c h) -> p c h", c=CHUNKS),
                                ALU.subtract).then_inc(s_shifted, 1)

            def weigh(i, b):
                dve.wait_ge(s_exp, RING * i + b + 1)
                g = gathered[:, b, :, 0:HF].rearrange("p c (h d) -> p c h d", h=H)
                v.tensor_tensor(g, g, gathered[:, b, :, HF:].unsqueeze(3).to_broadcast([P, CHUNKS, H, HD]),
                                ALU.mult).then_inc(s_weighted, 1)

            def normalise(i, b):
                t = RING * i + b
                link = chain(s_nm, t, NM)
                dve.wait_ge(s_agg, t + 1)
                link(v.tensor_single_scalar(denom[:], ps_agg[:, b % 2, HF:ROW], 0.5, ALU.max))
                link(v.reciprocal(rdenom[:], denom[:]))
                dve.wait_ge(s_stored[b], 16 * (i + 1))
                v.tensor_tensor(out_tile[:, b, :].rearrange("p (h d) -> p h d", h=H),
                                ps_agg[:, b % 2, 0:HF].rearrange("p (h d) -> p h d", h=H),
                                rdenom[:].unsqueeze(2).to_broadcast([P, H, HD]), ALU.mult).then_inc(s_normed, 1)

            def attend(i, first):
                for b in range(RING):
                    behind, two = lagged(i, b, 2), b >= 2 or not first
                    t = GROUPS + PICKS * i + b
                    link = chain(s_pick, t, PICK)
                    one_hot(i, b)
                    if two:
                        scores(*behind)
                    if b < PICKS:
                        pick_words(t, link)
                    edge_list(i, b)
                    if two:
                        row_maximum(*behind)
                    if b < PICKS:
                        split_words(t, link)
                    if two:
                        shift(*behind)
                    if b >= 3 or not first:
                        normalise(*lagged(i, b, 3))
                    if two:
                        weigh(*behind)

            attend(0, True)
            with dve.Fori(1, ROUNDS) as i:
                attend(i, False)
            for b in range(2, RING):
                scores(ROUNDS - 1, b)
                row_maximum(ROUNDS - 1, b)
                shift(ROUNDS - 1, b)
                normalise(ROUNDS - 1, b - 1)
                weigh(ROUNDS - 1, b)
            normalise(ROUNDS - 1, RING - 1)

            v.tensor_reduce(missed[:, 0:1], adj_sum[:], AX_X, ALU.add).then_inc(s_check, 1)
            v.tensor_reduce(missed[:, 1:2], empty_sum[:], AX_X, ALU.add).then_inc(s_check, 1)
            dve.wait_ge(s_check, 2)
            v.scalar_tensor_tensor(missed[:, 2:3], missed[:, 1:2], 1.0 / EMPTY, missed[:, 0:1], ALU.mult,
                                   ALU.add).then_inc(s_check, 1)
            dve.wait_ge(s_check, 3)
            v.tensor_single_scalar(missed[:, 3:4], missed[:, 2:3], -float(CHUNKS * TILES),
                                   ALU.add).then_inc(s_check, 1)
            dve.wait_ge(s_missed, 1)
            v.tensor_single_scalar(flag[:], ps_agg[0:1, 0, 0:1], 0.0, ALU.not_equal).then_inc(s_flag, 1)
            dve.wait_ge(s_flag, 1)
            with dve.If(dve.value_load(flag[0:1, 0:1], min_val=0, max_val=1) > 0):
                LINKS = [8, 8]

                def dense_scores(i, c, second, link):
                    n = 2 * TILES * i + TILES * second + c
                    v.tensor_copy(dn_adjf, dn_adj[:, bass.ds(c * P, P)])
                    v.tensor_tensor(dn_diag, ident[:].unsqueeze(1).to_broadcast([P, H, P]),
                                    node[:, bass.ds(c, 1), 0:H].rearrange("p o h -> p h o").to_broadcast([P, H, P]),
                                    ALU.mult).then_inc(d_diag, 1)
                    dve.wait_ge(d_f1, n + 1)
                    link(v.tensor_tensor(dn_s, ps_f1, node[:, bass.ds(i, 1), H:].rearrange(
                        "p o h -> p h o").to_broadcast([P, H, P]), ALU.add))
                    link(v.scalar_tensor_tensor(dn_s, dn_s, SLOPE, dn_s, ALU.mult, ALU.max))
                    link(v.tensor_tensor(dn_s, dn_s, dn_adjf.unsqueeze(1).to_broadcast([P, H, P]), ALU.mult))
                    link(v.tensor_scalar(dn_zero, dn_s, 0.0, NEG, ALU.is_equal, ALU.mult))
                    link(v.tensor_tensor(dn_s, dn_s, dn_zero, ALU.add))

                def chain(at, second):
                    n = [0]

                    def link(ins):
                        n[0] += 1
                        ins.then_inc(d_chain[second], 1)
                        dve.wait_ge(d_chain[second], LINKS[second] * at + n[0])
                    return n, link

                with dve.Fori(0, TILES) as i:
                    v.memset(dn_acc, 0.0).then_inc(d_tail, 1)
                    v.memset(dn_den, 0.0).then_inc(d_tail, 1)
                    v.memset(dn_max, NEG).then_inc(d_tail, 1)
                    dve.wait_ge(d_tail, 6 * i + 3)
                    dve.sem_inc(d_init)
                    dve.sem_inc(d_acc)
                    dve.wait_ge(d_adj_in, 16 * (i + 1))
                    dve.sem_inc(s_gate_dve)
                    with dve.Fori(0, TILES) as c:
                        n, link = chain(TILES * i + c, 0)
                        dense_scores(i, c, 0, link)
                        link(v.tensor_reduce(dn_part, dn_s, AX_X, ALU.max))
                        link(v.tensor_tensor(dn_max, dn_max, dn_part, ALU.max))
                        link(v.scalar_tensor_tensor(dn_ref, dn_max, 0.1 * NEG, dn_max, ALU.is_gt, ALU.mult))
                        assert n[0] == LINKS[0]
                    with dve.Fori(0, TILES) as c:
                        at = TILES * i + c
                        n, link = chain(at, 1)
                        dense_scores(i, c, 1, link)
                        v.tensor_tensor(dn_s, dn_s, dn_ref.unsqueeze(2).to_broadcast([P, H, P]),
                                        ALU.subtract).then_inc(d_shift, 1)
                        dve.wait_ge(d_exp, at + 1)
                        link(v.tensor_reduce(dn_part, dn_e, AX_X, ALU.add))
                        link(v.tensor_tensor(dn_den, dn_den, dn_part, ALU.add))
                        dve.wait_ge(d_part, at + 1)
                        link(v.tensor_tensor(dn_acc, dn_acc, ps_agg[:, 0, 0:HF], ALU.add))
                        assert n[0] == LINKS[1]
                        dve.sem_inc(d_acc)
                    v.tensor_single_scalar(dn_den, dn_den, 0.5, ALU.max).then_inc(d_tail, 1)
                    dve.wait_ge(d_tail, 6 * i + 4)
                    v.reciprocal(dn_rden, dn_den).then_inc(d_tail, 1)
                    dve.wait_ge(d_tail, 6 * i + 5)
                    v.tensor_tensor(dn_acc.rearrange("p (h d) -> p h d", h=H), dn_acc.rearrange("p (h d) -> p h d", h=H),
                                    dn_rden.unsqueeze(2).to_broadcast([P, H, HD]), ALU.mult).then_inc(d_tail, 1)
                    dve.wait_ge(d_tail, 6 * i + 6)
                    v.tensor_tensor(out_tile[:, 0, :], dn_acc,
                                    base[:, bass.ds(i, 1), :].rearrange("p o d -> p (o d)"), ALU.add).then_inc(d_out, 1)
                    dve.wait_ge(d_stored, 16 * (i + 1))


def kernel(x, adj, L0_gnn_weight, L0_gnn_weight_u, L0_gnn_weight_v, L0_gnn_bias, L0_gnn_proj_w, L0_gnn_proj_b):
    import numpy as _np
    import concourse.bacc as _bacc
    from concourse import mybir as _mybir
    from concourse.bass_utils import run_bass_kernel_spmd as _run

    nc = _bacc.Bacc("TRN2", target_bir_lowering=False, num_devices=1)
    given = {"x": x, "adj": adj, "weight": L0_gnn_weight, "weight_u": L0_gnn_weight_u,
             "weight_v": L0_gnn_weight_v, "bias": L0_gnn_bias,
             "proj_wT": _np.asarray(L0_gnn_proj_w).T, "proj_b": L0_gnn_proj_b}
    arrays, args = {}, []
    for name, a in given.items():
        a = _np.ascontiguousarray(a)
        arrays[f"in_{name}"] = a
        args.append(nc.dram_tensor(f"in_{name}", a.shape, _mybir.dt.from_np(a.dtype), kind="ExternalInput").ap())
    out = nc.dram_tensor("out", tuple(x.shape), F32, kind="ExternalOutput").ap()
    gat_kernel(nc, *args, out)
    r = _run(nc, [arrays], core_ids=[0])
    return r.results[0]["out"]
```

```python
from contextlib import ExitStack

import concourse.bass as bass
from concourse import mybir

ALU = mybir.AluOpType
ACT = mybir.ActivationFunctionType
F32 = mybir.dt.float32
BF16 = mybir.dt.bfloat16
I32 = mybir.dt.int32
U32 = mybir.dt.uint32
AX_X = mybir.AxisListType.X

P = 128
SLOTS = 16
CHUNKS = 5
EDGES = CHUNKS * P
BITS = 8
RING = 4
PICKS = 3
GROUP = 4
EMPTY = float(2 ** 20)
NEG = -1e30
SLOPE = 0.2
EPS = 1e-5


def gat_kernel(nc, x, adj, weight, weight_u, weight_v, bias, proj_wT, proj_b, out):
    N, D = x.shape
    H, HD = weight_u.shape[0], weight_u.shape[1]
    HF = H * HD
    KC = D // P
    TILES = N // P
    WORDS = N // BITS
    ROWS_STEP = P // BITS
    UNITS = 4
    UT = BITS // UNITS
    BANKS = WORDS // 512
    CANDS = 64
    SEG = WORDS // (CANDS // 8)
    ROW = HF + H
    STAGE = 2 * HF + 2 * H
    GROUPS = TILES // GROUP
    ROUNDS = TILES // RING
    assert GROUPS + PICKS * ROUNDS == TILES
    R_OFF, R_MID, R_ROW, R_F2 = SLOTS, SLOTS + 1, SLOTS + 2, SLOTS + 3
    REC = R_F2 + H

    with ExitStack() as ctx:
        def sb(name, shape, dt=F32):
            return ctx.enter_context(nc.sbuf_tensor(name, shape, dt))

        def ps(name, shape):
            return ctx.enter_context(nc.psum_tensor(name, shape, F32))

        def sem(name):
            return ctx.enter_context(nc.semaphore(name))

        table = nc.dram_tensor("support_table", (N, ROW), F32, kind="Internal").ap()

        adj_raw = sb("adj_raw", [P, UNITS, UT, WORDS], I32)
        adj_bf = sb("adj_bf", [P, UNITS, UT, WORDS], BF16)
        base = sb("base", [P, TILES, HF])
        node = sb("node", [P, TILES, 2 * H])
        record = sb("record", [P, TILES, REC])
        slot_pen = sb("slot_pen", [P, TILES, SLOTS])
        reach = sb("reach", [P, TILES])
        adj_sum = sb("adj_sum", [P, TILES * UNITS])
        out_tile = sb("out_tile", [P, RING, HF])
        EW = CHUNKS * ROW
        att = sb("att", [P, RING * (EW + 2 * EDGES)])
        gathered = att[:, 0:RING * EW].rearrange("p (b c r) -> p b c r", b=RING, c=CHUNKS)
        onehot = att[:, RING * EW:RING * (EW + EDGES)].rearrange("p (b e) -> p b e", b=RING)
        onehotT = att[:, RING * (EW + EDGES):].rearrange("p (b c r) -> p b c r", b=RING, c=CHUNKS)
        XN = 2 * GROUP * D
        x_in = att[:, 0:XN].rearrange("p (b i d) -> p b i d", b=2, i=GROUP)
        xhat = att[:, XN:2 * XN].rearrange("p (b i d) -> p b i d", b=2, i=GROUP)
        stage = att[:, 2 * XN:2 * XN + 2 * GROUP * STAGE].rearrange("p (b i d) -> p b i d", b=2, i=GROUP)
        uv_tmp = out_tile[:].rearrange("p (q c) d -> p q c d", q=2)
        ident = sb("ident", [P, P])
        ones_f = sb("ones_f", [P, P])
        before = sb("before", [P, P])
        minus_mid = sb("minus_mid", [P, P])
        w_all = sb("w_all", [P, KC, 2 * HF])
        w_uv = sb("w_uv", [P, KC, 2 * H])
        uv_row = sb("uv_row", [P, 2, HF])
        bias_row = sb("bias_row", [P, HF])
        projb_row = sb("projb_row", [P, HF])
        eps_col = sb("eps_col", [P, 1])
        pack_w = sb("pack_w", [P, BITS, P], BF16)
        pack_i = sb("pack_i", [P, 1], I32)
        pack_blk = sb("pack_blk", [P, ROWS_STEP])
        ones_row = sb("ones_row", [1, P], BF16)
        place_lo = sb("place_lo", [1, WORDS], BF16)
        place_hi = sb("place_hi", [1, WORDS], BF16)
        bit_shift = sb("bit_shift", [P, BITS], I32)
        bit_first = sb("bit_first", [P, BITS])
        edge_odd = sb("edge_odd", [P, EDGES])
        edge_at = sb("edge_at", [P, CHUNKS])
        slot_no = sb("slot_no", [P, SLOTS])
        row_no = sb("row_no", [P, P])
        hT = sb("hT", [P, 2, KC * P])
        stats = sb("stats", [P, GROUP, 6])
        mean_var = sb("mean_var", [P, GROUP, 2])
        std = sb("std", [P, GROUP])
        rstd = sb("rstd", [P, GROUP])
        cand = sb("cand", [P, CANDS])
        cand_rest = sb("cand_rest", [P, CANDS])
        words = sb("words", [P, SLOTS])
        words_i = sb("words_i", [P, SLOTS], I32)
        place_i = sb("place_i", [P, SLOTS], I32)
        bits = sb("bits", [P, SLOTS, BITS], I32)
        codes = sb("codes", [P, SLOTS, BITS])
        codes_rest = sb("codes_rest", [P, SLOTS * BITS])
        nbr = sb("nbr", [P, SLOTS])
        used = sb("used", [P, SLOTS])
        degree = sb("degree", [P, 1])
        distance = sb("distance", [P, EDGES])
        edge_rec = sb("edge_rec", [P, RING, CHUNKS, REC])
        edge_slot = sb("edge_slot", [P, CHUNKS])
        slot_hot = sb("slot_hot", [P, RING, CHUNKS, SLOTS])
        slot_nbr = sb("slot_nbr", [P, CHUNKS, SLOTS])
        edge_nbr = sb("edge_nbr", [P, CHUNKS])
        empty = sb("empty", [P, RING, CHUNKS])
        empty_sum = sb("empty_sum", [P, CHUNKS])
        idx = sb("idx", [P, RING, CHUNKS], U32)
        empty_pen = sb("empty_pen", [P, RING, CHUNKS])
        f2_edge = sb("f2_edge", [P, RING, CHUNKS, H])
        score = sb("score", [P, 2, CHUNKS, H])
        zero_pen = sb("zero_pen", [P, CHUNKS, H])
        score_slot = sb("score_slot", [P, CHUNKS, SLOTS, H])
        row_score = sb("row_score", [P, SLOTS, H])
        row_max = sb("row_max", [P, H])
        row_ref = sb("row_ref", [P, H])
        shifted = sb("shifted", [P, CHUNKS, H])
        denom = sb("denom", [P, H])
        rdenom = sb("rdenom", [P, H])

        ps_words = ps("ps_words", [P, WORDS])
        ps_agg = ps("ps_agg", [P, 2, 512])
        ps_off = ps("ps_off", [P, 512])
        ps_rec = ps("ps_rec", [P, 512])
        ps_row = ps("ps_row", [P, 512])
        ps_ref = ps("ps_ref", [P, 512])
        ps_t = [ps_off, ps_rec]
        ps_f = [ps_row, ps_ref]

        s_w_in = sem("weights_in")
        s_uv = sem("weight_uv_ready")
        s_uv_mul = sem("weight_uv_products")
        s_pool_const = sem("pool_constants")
        s_dve_const = sem("dve_constants")
        s_pack_i = sem("pack_weights_value")
        s_gate_dve = sem("gate_dve")
        s_gate_pool = sem("gate_pool")
        s_x_in = [sem(f"x_in{b}") for b in range(2)]
        s_bn = sem("bn_stats_done")
        s_stats = sem("mean_var_ready")
        s_std = sem("std_ready")
        s_rstd = sem("rstd_ready")
        s_xhat = sem("xhat_ready")
        s_xT = sem("xT_ready")
        s_hT = sem("hT_ready")
        s_proj = sem("projected")
        s_staged = sem("staged")
        s_basev = sem("base_partial")
        s_based = sem("base_ready")
        s_rows_out = [sem(f"table_rows_out{b}") for b in range(2)]
        s_adj_in = [sem(f"adj_in{u}") for u in range(UNITS)]
        s_conv = sem("converted")
        s_adj_used = sem("adj_bf_used")
        s_words_read = sem("words_read")
        s_pick = sem("pick_chain")
        s_nbr = sem("neighbours_ready")
        s_degree = sem("degree_ready")
        s_recorded = sem("neighbours_recorded")
        s_offset = sem("offset_ready")
        s_filed = sem("offset_recorded")
        s_distance = sem("distance_ready")
        s_onehot = sem("onehot_ready")
        s_rec = sem("edge_records_ready")
        s_rec_sb = sem("edge_records_in_sbuf")
        s_pen = sem("empty_penalty_ready")
        s_f2e = sem("edge_f2_ready")
        s_ls = sem("list_chain")
        s_idx = sem("idx_ready")
        s_gather = [sem(f"rows_gathered{b}") for b in range(RING)]
        s_onehotT = sem("onehotT_ready")
        s_sc = sem("score_chain")
        s_score = sem("slot_scores_ready")
        s_row = sem("row_scores_ready")
        s_mx = sem("max_chain")
        s_ref = sem("row_ref_ready")
        s_refe = sem("edge_ref_ready")
        s_shifted = sem("shifted_ready")
        s_exp = sem("exp_ready")
        s_weighted = sem("weighted_ready")
        s_agg = sem("aggregated")
        s_nm = sem("normalise_chain")
        s_normed = sem("normalised")
        s_out = sem("out_ready")
        s_stored = [sem(f"out_stored{b}") for b in range(RING)]
        s_check = sem("check_chain")
        s_missed = sem("missed_summed")
        s_flag = sem("flag_ready")
        d_init = sem("dense_tile_ready")
        d_adj_in = sem("dense_adj_in")
        d_diag = sem("dense_f1_diagonal")
        d_f1 = sem("dense_f1_spread")
        d_chain = [sem("dense_max_chain"), sem("dense_sum_chain")]
        d_shift = sem("dense_shifted")
        d_exp = sem("dense_exp")
        d_expT = sem("dense_exp_transposed")
        d_expT_sb = sem("dense_exp_transposed_in_sbuf")
        d_sup_in = sem("dense_support_in")
        d_part = sem("dense_partial_product")
        d_acc = sem("dense_accumulated")
        d_tail = sem("dense_tail_chain")
        d_out = sem("dense_out_ready")
        d_stored = sem("dense_out_stored")


        missed = sb("missed", [P, 4])
        flag = sb("flag", [1, 1], I32)
        dn_adj = adj_raw[:].rearrange("p u s e -> p (u s e)")
        dn_adjf = att[:, 0:P]
        dn_diag, dn_s, dn_zero, dn_e, dn_eT = (
            att[:, P + q * H * P:P + (q + 1) * H * P].rearrange("p (h m) -> p h m", h=H) for q in range(5))
        dn_rest = att[:, P + 5 * H * P:]
        dn_acc = dn_rest[:, 0:HF]
        dn_sup = dn_rest[:, HF:2 * HF]
        dn_max, dn_part, dn_ref, dn_den, dn_rden = (
            dn_rest[:, 2 * HF + q * H:2 * HF + (q + 1) * H] for q in range(5))
        ps_f1 = ps_words[:, 0:H * P].rearrange("p (h m) -> p h m", h=H)
        ps_eT = ps_words[:, 512:512 + H * P].rearrange("p (h m) -> p h m", h=H)

        adj_v = adj.rearrange("(T u s n) (m e) -> T u (n m) s e", u=UNITS, s=UT, n=ROWS_STEP, m=BITS)
        x_v = x.rearrange("(g i p) d -> g p i d", i=GROUP, p=P)
        table_v = table.rearrange("(g i p) d -> g p i d", i=GROUP, p=P)
        out_v = out.rearrange("(t p) d -> t p d", p=P)
        adj_rows = adj.rearrange("(t p) m -> t p m", p=P)
        table_rows = table[:, 0:HF].rearrange("(t p) d -> t p d", p=P)

        def lagged(i, b, lag):
            back = -((b - lag) // RING)
            return i - back, b - lag + back * RING

        block = ctx.enter_context(nc.Block())

        @block.sync
        def _(sp):
            def load_x(j, b, first):
                g = 2 * j + b
                if not first:
                    sp.wait_ge(s_xhat, GROUP * (g - 1))
                    sp.wait_ge(s_based, GROUP * (g - 1))
                sp.dma_start(x_in[:, b], x_v[g]).then_inc(s_x_in[b], 16)

            def load_adj(t, first=False):
                for u in range(UNITS):
                    if not first:
                        sp.wait_ge(s_conv, UNITS * (t - 1) + u + 1)
                    sp.dma_start(adj_raw[:, u], adj_v[t, u]).then_inc(s_adj_in[u], 16)

            load_x(0, 0, True)
            for dst, src in ((uv_row[:, 0, :], weight_u.rearrange("h d o -> o (h d)")),
                             (uv_row[:, 1, :], weight_v.rearrange("h d o -> o (h d)")),
                             (bias_row[:, :], bias),
                             (projb_row[:, :], proj_b.rearrange("(o d) -> o d", o=1))):
                sp.dma_start(dst, src.to_broadcast([P, HF])).then_inc(s_w_in, 16)
            for c in range(KC):
                sp.dma_start(w_all[:, c, 0:HF], proj_wT[c * P:(c + 1) * P, :]).then_inc(s_w_in, 16)
                sp.dma_start(w_all[:, c, HF:], weight[c * P:(c + 1) * P, :]).then_inc(s_w_in, 16)
            load_adj(0, True)
            load_x(0, 1, True)
            load_adj(1)
            with sp.Fori(1, GROUPS // 2) as j:
                for b in range(2):
                    load_adj(2 * j + b)
                    load_x(j, b, False)
            for b in range(RING):
                sp.sem_inc(s_stored[b], 16)

            with sp.Fori(GROUPS, TILES) as t:
                load_adj(t)
            for b in range(RING):
                sp.wait_ge(s_stored[b], 16 * (ROUNDS + 1))

            sp.wait_ge(s_flag, 1)
            with sp.If(sp.value_load(flag[0:1, 0:1], min_val=0, max_val=1) > 0):
                with sp.Fori(0, TILES) as i:
                    sp.wait_ge(d_init, i + 1)
                    sp.dma_start(dn_adj, adj_rows[i]).then_inc(d_adj_in, 16)
                    with sp.Fori(0, TILES) as c:
                        sp.wait_ge(d_acc, TILES * i + c + i + 1)
                        sp.dma_start(dn_sup, table_rows[c]).then_inc(d_sup_in, 16)
                    sp.wait_ge(d_out, i + 1)
                    sp.dma_start(out_v[i], out_tile[:, 0, :]).then_inc(d_stored, 16)
                sp.wait_ge(d_stored, 16 * TILES)

        @block.tensor
        def _(pe):
            def transposes(t, b, first):
                pe.wait_ge(s_xhat, t + 1)
                if not first:
                    pe.wait_ge(s_hT, t - 1)
                for c in range(KC):
                    mm = nc.tensor.transpose(ps_t[b % 2][:, c * P:(c + 1) * P],
                                             xhat[:, b // GROUP, b % GROUP, c * P:(c + 1) * P], ident[:])
                mm.then_inc(s_xT, 1)

            def project(t, b, first):
                pe.wait_ge(s_hT, t + 1)
                if not first:
                    pe.wait_ge(s_staged, t - 1)
                for c in range(KC):
                    nc.tensor.matmul(ps_agg[:, b % 2, :], hT[:, b % 2, c * P:(c + 1) * P], w_all[:, c, :],
                                     start=(c == 0), stop=(c == KC - 1))
                for c in range(KC):
                    mm = nc.tensor.matmul(ps_f[b % 2][:, 0:2 * H], hT[:, b % 2, c * P:(c + 1) * P],
                                          w_uv[:, c, :], start=(c == 0), stop=(c == KC - 1))
                mm.then_inc(s_proj, 1)

            def pack_places(t, first=False):
                if not first:
                    pe.wait_ge(s_words_read, t)
                for k in range(BANKS):
                    for row in (place_lo, place_hi):
                        nc.tensor.matmul(ps_words[:, k * 512:(k + 1) * 512], ones_row[:],
                                         row[:, k * 512:(k + 1) * 512], start=(row is place_lo), stop=False)

            def pack_unit(t, u):
                pe.wait_ge(s_conv, UNITS * t + u + 1)
                for s in range(UT):
                    for k in range(BANKS):
                        mm = nc.tensor.matmul(ps_words[:, k * 512:(k + 1) * 512], pack_w[:, u * UT + s, :],
                                              adj_bf[:, u, s, k * 512:(k + 1) * 512],
                                              start=False, stop=(u == UNITS - 1 and s == UT - 1))
                mm.then_inc(s_adj_used, 1)

            pe.wait_ge(s_pool_const, 7)
            pe.wait_ge(s_dve_const, 8)
            pack_places(0, True)
            for u in range(UNITS):
                pack_unit(0, u)
            pe.wait_ge(s_w_in, 16 * (2 * KC + 4))
            pe.wait_ge(s_uv, 4)

            def offsets(t, o):
                pe.wait_ge(s_degree, t + 1)
                nc.tensor.matmul(o[:, 0:1], before[:], degree[:], start=True, stop=True)
                nc.tensor.matmul(o[:, 1:2], minus_mid[:], degree[:], start=True, stop=True).then_inc(s_offset, 1)

            def tables(j, first):
                for gb in range(2):
                    g = 2 * j + gb
                    for q in range(GROUP + 1):
                        b = gb * GROUP + q
                        if q < GROUP:
                            transposes(2 * GROUP * j + b, b, first and b < 2)
                        if q > 0:
                            project(2 * GROUP * j + b - 1, b - 1, first and b - 1 < 2)
                        if q == 1:
                            pack_places(g + 1)
                        if q > 0:
                            pack_unit(g + 1, q - 1)
                    pe.wait_ge(s_staged, GROUP * g + GROUP - 1)
                    offsets(g, ps_f[0][:, 2 * H:])

            tables(0, True)
            with pe.Fori(1, GROUPS // 2) as j:
                tables(j, False)

            def edge_records(i, b):
                pe.wait_ge(s_onehot, RING * i + b + 1)
                for c in range(CHUNKS):
                    mm = nc.tensor.matmul(ps_rec[:, c * REC:(c + 1) * REC], onehot[:, b, c * P:(c + 1) * P],
                                          record[:, bass.ds(RING * i + b, 1), :].rearrange("p o r -> p (o r)"),
                                          start=True, stop=True)
                mm.then_inc(s_rec, 1)

            def row_scores(i, b):
                pe.wait_ge(s_onehotT, RING * i + b + 1)
                pe.wait_ge(s_score, RING * i + b + 1)
                for c in range(CHUNKS):
                    mm = nc.tensor.matmul(ps_row[:, 0:SLOTS * H], onehotT[:, b, c, :],
                                          score_slot[:, c].rearrange("p k h -> p (k h)"),
                                          start=(c == 0), stop=(c == CHUNKS - 1))
                mm.then_inc(s_row, 1)

            def edge_refs(i, b):
                pe.wait_ge(s_ref, RING * i + b + 1)
                for c in range(CHUNKS):
                    mm = nc.tensor.matmul(ps_ref[:, c * H:(c + 1) * H], onehot[:, b, c * P:(c + 1) * P],
                                          row_ref[:], start=True, stop=True)
                mm.then_inc(s_refe, 1)

            def aggregate(i, b):
                pe.wait_ge(s_weighted, RING * i + b + 1)
                for c in range(CHUNKS):
                    mm = nc.tensor.matmul(ps_agg[:, b % 2, 0:ROW], onehotT[:, b, c, :], gathered[:, b, c, :],
                                          start=(c == 0), stop=(c == CHUNKS - 1))
                mm.then_inc(s_agg, 1)

            pe.wait_ge(s_staged, TILES)

            def attend(i, first, last):
                for b in range(RING):
                    if last and b == RING - 1:
                        aggregate(*lagged(i, b, 4))
                    edge_records(i, b)
                    if b >= 3 or not first:
                        edge_refs(*lagged(i, b, 3))
                    if not first and not (last and b == RING - 1):
                        aggregate(*lagged(i, b, 4))
                    t = GROUPS + PICKS * i + b
                    packs = b < PICKS and not (last and b == PICKS - 1)
                    if packs:
                        pack_places(t + 1)
                        for u in range(UNITS // 2):
                            pack_unit(t + 1, u)
                    if b >= 2 or not first:
                        row_scores(*lagged(i, b, 2))
                    if b < PICKS and last:
                        offsets(t, ps_off)
                    if packs:
                        for u in range(UNITS // 2, UNITS):
                            pack_unit(t + 1, u)
                    if b < PICKS and not last:
                        offsets(t, ps_off)

            attend(0, True, False)
            with pe.Fori(1, ROUNDS - 1) as i:
                attend(i, False, False)
            attend(ROUNDS - 1, False, True)
            pe.wait_ge(s_check, 4)
            nc.tensor.matmul(ps_off[0:1, 0:1], missed[:, 3:4], ones_f[:, 0:1], start=True,
                             stop=True).then_inc(s_missed, 1)
            for b in range(RING):
                if b < 3:
                    edge_refs(*lagged(ROUNDS, b, 3))
                if b < 2:
                    row_scores(*lagged(ROUNDS, b, 2))
                aggregate(*lagged(ROUNDS, b, 4))

            pe.wait_ge(s_flag, 1)
            with pe.If(pe.value_load(flag[0:1, 0:1], min_val=0, max_val=1) > 0):
                def spread_f1(n):
                    pe.wait_ge(d_diag, n + 1)
                    nc.tensor.matmul(ps_f1, ones_f[:], dn_diag, start=True, stop=True).then_inc(d_f1, 1)

                with pe.Fori(0, TILES) as i:
                    with pe.Fori(0, TILES) as c:
                        spread_f1(2 * TILES * i + c)
                    with pe.Fori(0, TILES) as c:
                        spread_f1(2 * TILES * i + TILES + c)
                        pe.wait_ge(d_exp, TILES * i + c + 1)
                        for h in range(H):
                            mm = nc.tensor.transpose(ps_eT[:, h, :], dn_e[:, h, :], ident[:])
                        mm.then_inc(d_expT, 1)
                        pe.wait_ge(d_sup_in, 16 * (TILES * i + c + 1))
                        pe.wait_ge(d_expT_sb, TILES * i + c + 1)
                        for h in range(H):
                            mm = nc.tensor.matmul(ps_agg[:, 0, h * HD:(h + 1) * HD], dn_eT[:, h, :],
                                                  dn_sup[:, h * HD:(h + 1) * HD], start=True, stop=True)
                        mm.then_inc(d_part, 1)

        @block.scalar
        def _(act):
            def convert(t, units, first=False):
                for u in units:
                    act.wait_ge(s_adj_in[u], 16 * (t + 1))
                    if not first:
                        act.wait_ge(s_adj_used, UNITS * (t - 1) + u + 1)
                    nc.scalar.activation(adj_bf[:, u], adj_raw[:, u], ACT.Copy,
                                         accum_out=adj_sum[:, bass.ds(UNITS * t + u, 1)]).then_inc(s_conv, 1)

            def record_nbrs(t):
                act.wait_ge(s_nbr, t + 1)
                nc.scalar.activation(record[:, bass.ds(t, 1), 0:SLOTS].rearrange("p o k -> p (o k)"), nbr[:], ACT.Copy)
                nc.scalar.activation(used[:], nbr[:], ACT.Sign, accum_out=degree[:]).then_inc(s_degree, 1)
                act.wait_ge(s_degree, t + 1)
                nc.scalar.activation(slot_pen[:, bass.ds(t, 1), :].rearrange("p o k -> p (o k)"), used[:], ACT.Copy,
                                     scale=-NEG, bias=NEG)
                nc.scalar.activation(reach[:, bass.ds(t, 1)], degree[:], ACT.Square, scale=0.5).then_inc(s_recorded, 1)

            def record_offset(t, o):
                act.wait_ge(s_offset, t + 1)
                nc.scalar.activation(record[:, bass.ds(t, 1), R_OFF:R_MID + 1].rearrange("p o k -> p (o k)"),
                                     o[:, 0:2], ACT.Copy).then_inc(s_filed, 1)

            def deviation(g):
                act.wait_ge(s_stats, g + 1)
                nc.scalar.activation(std[:], mean_var[:, :, 1], ACT.Sqrt, bias=eps_col[:, 0:1]).then_inc(s_std, 1)

            def tables(j, first, last):
                for gb in range(2):
                    g = 2 * j + gb
                    if not first:
                        act.wait_ge(s_based, GROUP * (g - 1))
                        act.wait_ge(s_rows_out[gb], 16 * j)
                    for q in range(GROUP + 1):
                        b = gb * GROUP + q
                        t = 2 * GROUP * j + b
                        if q == 0 and not (first and gb == 0):
                            record_offset(g - 1, ps_f[0][:, 2 * H:])
                        if q < GROUP:
                            act.wait_ge(s_xT, t + 1)
                            if not (first and b < 2):
                                act.wait_ge(s_proj, t - 1)
                            nc.scalar.activation(hT[:, b % 2, :], ps_t[b % 2][:, 0:KC * P],
                                                 ACT.Relu).then_inc(s_hT, 1)
                        if q > 0:
                            act.wait_ge(s_proj, t)
                            nc.scalar.activation(stage[:, gb, q - 1, 0:2 * HF], ps_agg[:, (b - 1) % 2, :],
                                                 ACT.Copy)
                            nc.scalar.activation(stage[:, gb, q - 1, 2 * HF:STAGE], ps_f[(b - 1) % 2][:, 0:2 * H],
                                                 ACT.Copy).then_inc(s_staged, 1)
                        if q < GROUP:
                            convert(g + 1, [q])
                        if q == 2 and not (last and gb == 1):
                            deviation(g + 1)
                        if q == 3:
                            record_nbrs(g)
                    act.wait_ge(s_staged, GROUP * (g + 1))
                    act.dma_start(table_v[g], stage[:, gb, :, HF:HF + ROW]).then_inc(s_rows_out[gb], 16)

            act.wait_ge(s_dve_const, 8)
            convert(0, range(UNITS), True)
            deviation(0)
            tables(0, True, False)
            with act.Fori(1, GROUPS // 2 - 1) as j:
                tables(j, False, False)
            tables(GROUPS // 2 - 1, False, True)

            def exponential(i, b):
                act.wait_ge(s_shifted, RING * i + b + 1)
                nc.scalar.activation(gathered[:, b, :, HF:], shifted[:], ACT.Exp).then_inc(s_exp, 1)

            def distances(i, b, first=False):
                t = RING * i + b
                act.wait_ge(s_filed, t + 1)
                if not first:
                    act.wait_ge(s_onehot, t)
                nc.scalar.activation(distance[:], edge_odd[:], ACT.Square, scale=0.5,
                                     bias=record[:, bass.ds(t, 1), R_MID:R_MID + 1].rearrange(
                                         "p o k -> p (o k)")).then_inc(s_distance, 1)

            def record_edges(i, b):
                act.wait_ge(s_rec, RING * i + b + 1)
                nc.scalar.activation(edge_rec[:, b].rearrange("p c r -> p (c r)"), ps_rec[:, 0:CHUNKS * REC],
                                     ACT.Copy).then_inc(s_rec_sb, 1)

            def store_out(i, b):
                act.wait_ge(s_out, RING * i + b + 1)
                act.dma_start(out_v[RING * i + b], out_tile[:, b, :]).then_inc(s_stored[b], 16)

            def attend(i, first=False, second=False, last=False):
                for b in range(RING):
                    t = GROUPS + PICKS * i + b
                    begin = PICKS if b == 0 else UNITS * b
                    end = UNITS * (PICKS - 1) if last else UNITS * PICKS + PICKS
                    units = [(GROUPS + PICKS * i + 1 + k // UNITS, k % UNITS)
                             for k in range(begin, min(UNITS * (b + 1), end))]
                    next_tile = (i, b + 1) if b < RING - 1 else (i + 1, 0)
                    for tile, u in units[0:1]:
                        convert(tile, [u])
                    if b > 0 and not last:
                        record_offset(t - 1, ps_off)
                    record_edges(i, b)
                    if not last:
                        distances(*next_tile)
                    for tile, u in units[1:2]:
                        convert(tile, [u])
                    if b >= 3 or not first:
                        exponential(*lagged(i, b, 3))
                    for tile, u in units[2:]:
                        convert(tile, [u])
                    if b < PICKS:
                        record_nbrs(t)
                    if last and b < PICKS:
                        record_offset(t, ps_off)
                        distances(*next_tile)
                    if not first and not (second and b < 2):
                        store_out(*lagged(i, b, 6))

            record_offset(GROUPS - 1, ps_f[0][:, 2 * H:])
            distances(0, 0, True)
            convert(GROUPS + 1, range(PICKS))
            attend(0, first=True)
            attend(1, second=True)
            with act.Fori(2, ROUNDS - 1) as i:
                attend(i)
            attend(ROUNDS - 1, last=True)
            for b in range(3):
                exponential(*lagged(ROUNDS, b, 3))
                store_out(*lagged(ROUNDS, b, 6))
            for b in range(3, 6):
                store_out(*lagged(ROUNDS, b, 6))

            act.wait_ge(s_flag, 1)
            with act.If(act.value_load(flag[0:1, 0:1], min_val=0, max_val=1) > 0):
                with act.Fori(0, TILES * TILES) as n:
                    act.wait_ge(d_shift, n + 1)
                    nc.scalar.activation(dn_e, dn_s, ACT.Exp).then_inc(d_exp, 1)
                    act.wait_ge(d_expT, n + 1)
                    nc.scalar.activation(dn_eT, ps_eT, ACT.Copy).then_inc(d_expT_sb, 1)

        @block.gpsimd
        def _(pool):
            ramp = dict(allow_small_or_imprecise_dtypes=True)
            pool.memset(ident[:], 0.0).then_inc(s_pool_const, 1)
            pool.memset(pack_blk[:], 1.0).then_inc(s_pool_const, 1)
            pool.iota(pack_i[:], [[0, 1]], base=0, channel_multiplier=1).then_inc(s_pool_const, 1)
            pool.iota(place_lo[:], [[0, WORDS // 256], [1, 256]], base=0, channel_multiplier=0,
                      **ramp).then_inc(s_pool_const, 1)
            pool.iota(place_hi[:], [[256, WORDS // 256], [0, 256]], base=0, channel_multiplier=0,
                      **ramp).then_inc(s_pool_const, 1)
            pool.wait_ge(s_pool_const, 5)
            pool.affine_select(pack_blk[:], pack_blk[:], [[-BITS, ROWS_STEP]], ALU.is_ge, 0.0, base=0,
                               channel_multiplier=1).then_inc(s_pool_const, 1)
            pool.wait_ge(s_pool_const, 6)
            pool.affine_select(pack_blk[:], pack_blk[:], [[BITS, ROWS_STEP]], ALU.is_ge, 0.0, base=BITS - 1,
                               channel_multiplier=-1).then_inc(s_pool_const, 1)
            pool.iota(bit_shift[:], [[1, BITS]], base=WORDS.bit_length() - 1,
                      channel_multiplier=0).then_inc(s_pool_const, 1)
            pool.iota(bit_first[:], [[WORDS, BITS]], base=1, channel_multiplier=0, **ramp).then_inc(s_pool_const, 1)
            pool.affine_select(ident[:], ident[:], [[-1, P]], ALU.not_equal, 1.0, base=0,
                               channel_multiplier=1).then_inc(s_pool_const, 1)
            pool.memset(before[:], 1.0).then_inc(s_pool_const, 1)
            pool.wait_ge(s_pool_const, 11)
            pool.affine_select(before[:], before[:], [[1, P]], ALU.is_gt, 0.0, base=0,
                               channel_multiplier=-1).then_inc(s_pool_const, 1)
            pool.iota(edge_odd[:], [[2, EDGES]], base=1, channel_multiplier=0, **ramp).then_inc(s_pool_const, 1)
            pool.iota(edge_at[:], [[P, CHUNKS]], base=0, channel_multiplier=1, **ramp).then_inc(s_pool_const, 1)
            pool.iota(slot_no[:], [[1, SLOTS]], base=0, channel_multiplier=0, **ramp).then_inc(s_pool_const, 1)
            pool.iota(row_no[:], [[1, P]], base=1, channel_multiplier=0, **ramp).then_inc(s_pool_const, 1)
            pool.iota(record[:, :, R_ROW], [[0, TILES]], base=1, channel_multiplier=1,
                      **ramp).then_inc(s_pool_const, 1)
            pool.wait_ge(s_w_in, 16 * (2 * KC + 4))
            pool.tensor_tensor(bias_row[:], bias_row[:], projb_row[:], ALU.add).then_inc(s_pool_const, 1)
            pool.wait_ge(s_pool_const, 18)

            def tables(j):
                for gb in range(2):
                    pool.wait_ge(s_x_in[gb], 16 * (j + 1))
                    for q in range(GROUP):
                        t = GROUP * (2 * j + gb) + q
                        bt = base[:, bass.ds(t, 1), :].rearrange("p o d -> p (o d)")
                        pool.tensor_tensor(bt, x_in[:, gb, q, :], bias_row[:], ALU.add).then_inc(s_basev, 1)
                        pool.wait_ge(s_staged, t + 1)
                        pool.wait_ge(s_basev, t + 1)
                        pool.tensor_copy(node[:, bass.ds(t, 1), :].rearrange("p o d -> p (o d)"),
                                         stage[:, gb, q, 2 * HF:STAGE])
                        pool.tensor_copy(record[:, bass.ds(t, 1), R_F2:].rearrange("p o d -> p (o d)"),
                                         stage[:, gb, q, 2 * HF + H:STAGE])
                        pool.tensor_tensor(bt, bt, stage[:, gb, q, 0:HF], ALU.add).then_inc(s_based, 1)

            with pool.Fori(0, GROUPS // 2) as j:
                tables(j)

            for b in range(2):
                pool.wait_ge(s_rows_out[b], 16 * (GROUPS // 2))
            pool.wait_ge(s_xhat, TILES)
            pool.wait_ge(s_xT, TILES)
            pool.memset(att[:, 0:RING * EW], 0.0).then_inc(s_pool_const, 1)
            pool.wait_ge(s_pool_const, 19)

            def gather(i, b, first):
                t = RING * i + b
                pool.wait_ge(s_idx, t + 1)
                if not first:
                    pool.wait_ge(s_agg, t - RING + 1)
                pool.sem_inc(s_gate_pool)
                for c in range(CHUNKS):
                    pool.indirect_dma_start(gathered[:, b, c, :], None, table,
                                            bass.IndirectOffsetOnAxis(idx[:, b, c:c + 1], 0),
                                            bounds_check=N - 1, oob_is_err=False).then_inc(s_gather[b], 16)
                pool.tensor_scalar(empty_pen[:, b, :], edge_rec[:, b, :, R_ROW], 0.0, NEG, ALU.is_equal,
                                   ALU.mult).then_inc(s_pen, 1)
                for c in range(CHUNKS):
                    last = pool.tensor_scalar(onehotT[:, b, c, :], row_no[:], edge_rec[:, b, c, R_ROW:R_ROW + 1],
                                              None, ALU.is_equal)
                last.then_inc(s_onehotT, 1)
                pool.wait_ge(s_pen, t + 1)
                pool.tensor_tensor(f2_edge[:, b], empty_pen[:, b, :].unsqueeze(2).to_broadcast([P, CHUNKS, H]),
                                   edge_rec[:, b, :, R_F2:], ALU.add).then_inc(s_f2e, 1)

            def add_base(i, b):
                t = RING * i + b
                pool.wait_ge(s_normed, t + 1)
                pool.tensor_tensor(out_tile[:, b, :], out_tile[:, b, :],
                                   base[:, bass.ds(t, 1), :].rearrange("p o d -> p (o d)"), ALU.add).then_inc(s_out, 1)

            def attend(i, first):
                for b in range(RING):
                    gather(i, b, first)
                    if not first:
                        add_base(*lagged(i, b, 4))

            attend(0, True)
            with pool.Fori(1, ROUNDS) as i:
                attend(i, False)
            for b in range(RING):
                add_base(ROUNDS - 1, b)

        @block.vector
        def _(dve):
            v = nc.vector

            def chain(sem_, at, links):
                n = [0]

                def link(ins):
                    n[0] += 1
                    assert n[0] <= links
                    ins.then_inc(sem_, 1)
                    dve.wait_ge(sem_, links * at + n[0])
                return link

            v.memset(eps_col[:], EPS).then_inc(s_dve_const, 1)
            v.memset(ones_f[:], 1.0).then_inc(s_dve_const, 1)
            v.memset(ones_row[:], 1.0).then_inc(s_dve_const, 1)
            v.memset(empty_sum[:], 0.0).then_inc(s_dve_const, 1)
            v.memset(pack_w[:], 0.0).then_inc(s_dve_const, 1)
            dve.wait_ge(s_pool_const, 7)
            v.tensor_single_scalar(pack_i[:], pack_i[:], BITS - 1, ALU.bitwise_and).then_inc(s_dve_const, 1)
            dve.wait_ge(s_dve_const, 6)
            v.tensor_single_scalar(pack_i[:], pack_i[:], 127 + WORDS.bit_length() - 1, ALU.add).then_inc(s_dve_const, 1)
            dve.wait_ge(s_dve_const, 7)
            v.tensor_single_scalar(pack_i[:], pack_i[:], 23, ALU.logical_shift_left).then_inc(s_pack_i, 1)
            dve.wait_ge(s_pack_i, 1)
            for s in range(BITS):
                last = v.tensor_scalar(pack_w[:, s, s * ROWS_STEP:(s + 1) * ROWS_STEP], pack_blk[:],
                                       pack_i[:].bitcast(F32)[:, 0:1], None, ALU.mult)
            dve.wait_ge(s_pool_const, 12)
            v.scalar_tensor_tensor(minus_mid[:], ident[:], -0.5, before[:], ALU.mult,
                                   ALU.subtract).then_inc(s_dve_const, 1)
            dve.wait_ge(s_w_in, 16 * (2 * KC + 4))
            for q in range(2):
                for c in range(KC):
                    v.tensor_tensor(uv_tmp[:, q, c], w_all[:, c, HF:], uv_row[:, q, :], ALU.mult).then_inc(s_uv_mul, 1)
            dve.wait_ge(s_uv_mul, 2 * KC)
            for q in range(2):
                for c in range(KC):
                    v.tensor_reduce(w_uv[:, c, q * H:(q + 1) * H],
                                    uv_tmp[:, q, c].rearrange("p (h d) -> p h d", h=H), AX_X,
                                    ALU.add).then_inc(s_uv, 1)

            PICK = 9

            def pick_words(t, link):
                dve.wait_ge(s_adj_used, UNITS * (t + 1))
                dve.sem_inc(s_gate_dve)
                for s in range(CANDS // 8):
                    last = v.max(cand[:, s * 8:(s + 1) * 8], ps_words[:, s * SEG:(s + 1) * SEG])
                last.then_inc(s_words_read, 1)
                dve.wait_ge(s_words_read, t + 1)
                dve.sem_inc(s_gate_dve)
                link(v.max(words[:, 0:8], cand[:]))
                dve.sem_inc(s_gate_dve)
                link(v.match_replace(cand_rest[:], words[:, 0:8], cand[:], 0.0))
                dve.sem_inc(s_gate_dve)
                link(v.max(words[:, 8:16], cand_rest[:]))

            def split_words(t, link, first=False):
                link(v.tensor_copy(words_i[:], words[:]))
                v.tensor_tensor(bits[:], words_i[:].unsqueeze(2).to_broadcast([P, SLOTS, BITS]),
                                bit_shift[:].unsqueeze(1).to_broadcast([P, SLOTS, BITS]), ALU.logical_shift_right)
                link(v.tensor_single_scalar(place_i[:], words_i[:], WORDS - 1, ALU.bitwise_and))
                v.tensor_tensor(codes[:], place_i[:].unsqueeze(2).to_broadcast([P, SLOTS, BITS]),
                                bit_first[:].unsqueeze(1).to_broadcast([P, SLOTS, BITS]), ALU.add)
                link(v.tensor_single_scalar(bits[:], bits[:], 1, ALU.bitwise_and))
                link(v.tensor_tensor(codes[:], codes[:], bits[:], ALU.mult))
                codes_f = codes[:].rearrange("p k b -> p (k b)")
                if not first:
                    dve.wait_ge(s_recorded, t)
                dve.sem_inc(s_gate_dve)
                link(v.max(nbr[:, 0:8], codes_f))
                dve.sem_inc(s_gate_dve)
                link(v.match_replace(codes_rest[:], nbr[:, 0:8], codes_f, 0.0))
                dve.sem_inc(s_gate_dve)
                v.max(nbr[:, 8:16], codes_rest[:]).then_inc(s_nbr, 1)

            dve.wait_ge(s_pool_const, 18)

            def tables(j, first):
                for gb in range(2):
                    g = 2 * j + gb
                    link = chain(s_pick, g, PICK)
                    dve.wait_ge(s_x_in[gb], 16 * (j + 1))
                    for q in range(GROUP):
                        last = v.bn_stats(stats[:, q, :], x_in[:, gb, q, :])
                    last.then_inc(s_bn, 1)
                    dve.wait_ge(s_bn, g + 1)
                    dve.sem_inc(s_gate_dve)
                    for q in range(GROUP):
                        last = v.bn_aggr(mean_var[:, q, :], stats[:, q, :])
                    last.then_inc(s_stats, 1)
                    dve.wait_ge(s_stats, g + 1)
                    dve.wait_ge(s_std, g + 1)
                    v.reciprocal(rstd[:], std[:]).then_inc(s_rstd, 1)
                    dve.wait_ge(s_rstd, g + 1)
                    if not first:
                        dve.wait_ge(s_xT, GROUP * (g - 1))
                    for q in range(GROUP):
                        v.tensor_scalar(xhat[:, gb, q, :], x_in[:, gb, q, :], mean_var[:, q, 0:1],
                                        rstd[:, q:q + 1], ALU.subtract, ALU.mult).then_inc(s_xhat, 1)
                    pick_words(g, link)
                    split_words(g, link, first and gb == 0)

            tables(0, True)
            with dve.Fori(1, GROUPS // 2) as j:
                tables(j, False)
            dve.wait_ge(s_based, TILES)
            for b in range(2):
                dve.wait_ge(s_rows_out[b], 16 * (GROUPS // 2))

            LS, SC, MX, NM = 4, 4, 2, 2

            def one_hot(i, b):
                t = RING * i + b
                dve.wait_ge(s_distance, t + 1)
                v.tensor_scalar(onehot[:, b, :], distance[:], reach[:, bass.ds(t, 1)], None,
                                ALU.is_lt).then_inc(s_onehot, 1)

            def edge_list(i, b):
                t = RING * i + b
                link = chain(s_ls, t, LS)
                dve.wait_ge(s_rec_sb, t + 1)
                v.tensor_scalar(empty[:, b, :], edge_rec[:, b, :, R_ROW], 0.0, EMPTY, ALU.is_equal, ALU.mult)
                link(v.tensor_tensor(edge_slot[:], edge_at[:], edge_rec[:, b, :, R_OFF], ALU.subtract))
                v.tensor_tensor(empty_sum[:], empty_sum[:], empty[:, b, :], ALU.add)
                link(v.tensor_tensor(slot_hot[:, b], slot_no[:].unsqueeze(1).to_broadcast([P, CHUNKS, SLOTS]),
                                     edge_slot[:].unsqueeze(2).to_broadcast([P, CHUNKS, SLOTS]), ALU.is_equal))
                link(v.tensor_tensor(slot_nbr[:], slot_hot[:, b], edge_rec[:, b, :, 0:SLOTS], ALU.mult))
                link(v.tensor_reduce(edge_nbr[:], slot_nbr[:], AX_X, ALU.add))
                v.scalar_tensor_tensor(idx[:, b, :], edge_nbr[:], -1.0, empty[:, b, :], ALU.add,
                                       ALU.add).then_inc(s_idx, 1)

            def scores(i, b):
                t = RING * i + b
                link = chain(s_sc, t, SC)
                dve.wait_ge(s_gather[b], 16 * CHUNKS * (i + 1))
                dve.wait_ge(s_f2e, t + 1)
                link(v.tensor_tensor(score[:, b % 2], gathered[:, b, :, HF:], f2_edge[:, b], ALU.add))
                link(v.scalar_tensor_tensor(score[:, b % 2], score[:, b % 2], SLOPE, score[:, b % 2], ALU.mult, ALU.max))
                link(v.tensor_scalar(zero_pen[:], score[:, b % 2], 0.0, NEG, ALU.is_equal, ALU.mult))
                link(v.tensor_tensor(score[:, b % 2], score[:, b % 2], zero_pen[:], ALU.add))
                v.tensor_tensor(score_slot[:], slot_hot[:, b].unsqueeze(3).to_broadcast([P, CHUNKS, SLOTS, H]),
                                score[:, b % 2].unsqueeze(2).to_broadcast([P, CHUNKS, SLOTS, H]),
                                ALU.mult).then_inc(s_score, 1)

            def row_maximum(i, b):
                t = RING * i + b
                link = chain(s_mx, t, MX)
                dve.wait_ge(s_row, t + 1)
                link(v.tensor_tensor(row_score[:], ps_row[:, 0:SLOTS * H].rearrange("p (k h) -> p k h", k=SLOTS),
                                     slot_pen[:, bass.ds(t, 1), :].rearrange("p o k -> p k o").to_broadcast([P, SLOTS, H]), ALU.add))
                link(v.tensor_reduce(row_max[:], row_score[:].rearrange("p k h -> p h k"), AX_X, ALU.max))
                v.scalar_tensor_tensor(row_ref[:], row_max[:], 0.1 * NEG, row_max[:], ALU.is_gt,
                                       ALU.mult).then_inc(s_ref, 1)

            def shift(i, b):
                dve.wait_ge(s_refe, RING * i + b + 1)
                v.tensor_tensor(shifted[:], score[:, b % 2], ps_ref[:, 0:CHUNKS * H].rearrange("p (c h) -> p c h", c=CHUNKS),
                                ALU.subtract).then_inc(s_shifted, 1)

            def weigh(i, b):
                dve.wait_ge(s_exp, RING * i + b + 1)
                g = gathered[:, b, :, 0:HF].rearrange("p c (h d) -> p c h d", h=H)
                v.tensor_tensor(g, g, gathered[:, b, :, HF:].unsqueeze(3).to_broadcast([P, CHUNKS, H, HD]),
                                ALU.mult).then_inc(s_weighted, 1)

            def normalise(i, b):
                t = RING * i + b
                link = chain(s_nm, t, NM)
                dve.wait_ge(s_agg, t + 1)
                link(v.tensor_single_scalar(denom[:], ps_agg[:, b % 2, HF:ROW], 0.5, ALU.max))
                link(v.reciprocal(rdenom[:], denom[:]))
                dve.wait_ge(s_stored[b], 16 * (i + 1))
                v.tensor_tensor(out_tile[:, b, :].rearrange("p (h d) -> p h d", h=H),
                                ps_agg[:, b % 2, 0:HF].rearrange("p (h d) -> p h d", h=H),
                                rdenom[:].unsqueeze(2).to_broadcast([P, H, HD]), ALU.mult).then_inc(s_normed, 1)

            def attend(i, first, last=False):
                for b in range(RING):
                    t = GROUPS + PICKS * i + b
                    link = chain(s_pick, t, PICK)
                    one_hot(i, b)
                    if b >= 3 or not first:
                        row_maximum(*lagged(i, b, 3))
                    if b < PICKS:
                        pick_words(t, link)
                    if last:
                        edge_list(i, b)
                    if b >= 2 or not first:
                        scores(*lagged(i, b, 2))
                    if b >= 3 or not first:
                        shift(*lagged(i, b, 3))
                    if b < PICKS:
                        split_words(t, link)
                    if not last:
                        edge_list(i, b)
                    if b >= 3 or not first:
                        weigh(*lagged(i, b, 3))
                    if not first:
                        normalise(*lagged(i, b, 4))

            attend(0, True)
            with dve.Fori(1, ROUNDS - 1) as i:
                attend(i, False)
            attend(ROUNDS - 1, False, True)
            v.tensor_reduce(missed[:, 0:1], adj_sum[:], AX_X, ALU.add).then_inc(s_check, 1)
            v.tensor_reduce(missed[:, 1:2], empty_sum[:], AX_X, ALU.add).then_inc(s_check, 1)
            dve.wait_ge(s_check, 2)
            v.scalar_tensor_tensor(missed[:, 2:3], missed[:, 1:2], 1.0 / EMPTY, missed[:, 0:1], ALU.mult,
                                   ALU.add).then_inc(s_check, 1)
            dve.wait_ge(s_check, 3)
            v.tensor_single_scalar(missed[:, 3:4], missed[:, 2:3], -float(CHUNKS * TILES),
                                   ALU.add).then_inc(s_check, 1)
            for b in range(3):
                row_maximum(*lagged(ROUNDS, b, 3))
                if b < 2:
                    scores(*lagged(ROUNDS, b, 2))
                if b == 1:
                    dve.wait_ge(s_missed, 1)
                    v.tensor_single_scalar(flag[:], ps_off[0:1, 0:1], 0.0, ALU.not_equal).then_inc(s_flag, 1)
                if b > 0:
                    normalise(*lagged(ROUNDS, b, 5))
                shift(*lagged(ROUNDS, b, 3))
                weigh(*lagged(ROUNDS, b, 3))
            for b in range(3, 5):
                normalise(*lagged(ROUNDS, b, 5))

            dve.wait_ge(s_flag, 1)
            with dve.If(dve.value_load(flag[0:1, 0:1], min_val=0, max_val=1) > 0):
                LINKS = [8, 8]

                def dense_scores(i, c, second, link):
                    n = 2 * TILES * i + TILES * second + c
                    v.tensor_copy(dn_adjf, dn_adj[:, bass.ds(c * P, P)])
                    v.tensor_tensor(dn_diag, ident[:].unsqueeze(1).to_broadcast([P, H, P]),
                                    node[:, bass.ds(c, 1), 0:H].rearrange("p o h -> p h o").to_broadcast([P, H, P]),
                                    ALU.mult).then_inc(d_diag, 1)
                    dve.wait_ge(d_f1, n + 1)
                    link(v.tensor_tensor(dn_s, ps_f1, node[:, bass.ds(i, 1), H:].rearrange(
                        "p o h -> p h o").to_broadcast([P, H, P]), ALU.add))
                    link(v.scalar_tensor_tensor(dn_s, dn_s, SLOPE, dn_s, ALU.mult, ALU.max))
                    link(v.tensor_tensor(dn_s, dn_s, dn_adjf.unsqueeze(1).to_broadcast([P, H, P]), ALU.mult))
                    link(v.tensor_scalar(dn_zero, dn_s, 0.0, NEG, ALU.is_equal, ALU.mult))
                    link(v.tensor_tensor(dn_s, dn_s, dn_zero, ALU.add))

                def chain(at, second):
                    n = [0]

                    def link(ins):
                        n[0] += 1
                        ins.then_inc(d_chain[second], 1)
                        dve.wait_ge(d_chain[second], LINKS[second] * at + n[0])
                    return n, link

                with dve.Fori(0, TILES) as i:
                    v.memset(dn_acc, 0.0).then_inc(d_tail, 1)
                    v.memset(dn_den, 0.0).then_inc(d_tail, 1)
                    v.memset(dn_max, NEG).then_inc(d_tail, 1)
                    dve.wait_ge(d_tail, 6 * i + 3)
                    dve.sem_inc(d_init)
                    dve.sem_inc(d_acc)
                    dve.wait_ge(d_adj_in, 16 * (i + 1))
                    dve.sem_inc(s_gate_dve)
                    with dve.Fori(0, TILES) as c:
                        n, link = chain(TILES * i + c, 0)
                        dense_scores(i, c, 0, link)
                        link(v.tensor_reduce(dn_part, dn_s, AX_X, ALU.max))
                        link(v.tensor_tensor(dn_max, dn_max, dn_part, ALU.max))
                        link(v.scalar_tensor_tensor(dn_ref, dn_max, 0.1 * NEG, dn_max, ALU.is_gt, ALU.mult))
                        assert n[0] == LINKS[0]
                    with dve.Fori(0, TILES) as c:
                        at = TILES * i + c
                        n, link = chain(at, 1)
                        dense_scores(i, c, 1, link)
                        v.tensor_tensor(dn_s, dn_s, dn_ref.unsqueeze(2).to_broadcast([P, H, P]),
                                        ALU.subtract).then_inc(d_shift, 1)
                        dve.wait_ge(d_exp, at + 1)
                        link(v.tensor_reduce(dn_part, dn_e, AX_X, ALU.add))
                        link(v.tensor_tensor(dn_den, dn_den, dn_part, ALU.add))
                        dve.wait_ge(d_part, at + 1)
                        link(v.tensor_tensor(dn_acc, dn_acc, ps_agg[:, 0, 0:HF], ALU.add))
                        assert n[0] == LINKS[1]
                        dve.sem_inc(d_acc)
                    v.tensor_single_scalar(dn_den, dn_den, 0.5, ALU.max).then_inc(d_tail, 1)
                    dve.wait_ge(d_tail, 6 * i + 4)
                    v.reciprocal(dn_rden, dn_den).then_inc(d_tail, 1)
                    dve.wait_ge(d_tail, 6 * i + 5)
                    v.tensor_tensor(dn_acc.rearrange("p (h d) -> p h d", h=H), dn_acc.rearrange("p (h d) -> p h d", h=H),
                                    dn_rden.unsqueeze(2).to_broadcast([P, H, HD]), ALU.mult).then_inc(d_tail, 1)
                    dve.wait_ge(d_tail, 6 * i + 6)
                    v.tensor_tensor(out_tile[:, 0, :], dn_acc,
                                    base[:, bass.ds(i, 1), :].rearrange("p o d -> p (o d)"), ALU.add).then_inc(d_out, 1)
                    dve.wait_ge(d_stored, 16 * (i + 1))


def kernel(x, adj, L0_gnn_weight, L0_gnn_weight_u, L0_gnn_weight_v, L0_gnn_bias, L0_gnn_proj_w, L0_gnn_proj_b):
    import numpy as _np
    import concourse.bacc as _bacc
    from concourse import mybir as _mybir
    from concourse.bass_utils import run_bass_kernel_spmd as _run

    nc = _bacc.Bacc("TRN2", target_bir_lowering=False, num_devices=1)
    given = {"x": x, "adj": adj, "weight": L0_gnn_weight, "weight_u": L0_gnn_weight_u,
             "weight_v": L0_gnn_weight_v, "bias": L0_gnn_bias,
             "proj_wT": _np.asarray(L0_gnn_proj_w).T, "proj_b": L0_gnn_proj_b}
    arrays, args = {}, []
    for name, a in given.items():
        a = _np.ascontiguousarray(a)
        arrays[f"in_{name}"] = a
        args.append(nc.dram_tensor(f"in_{name}", a.shape, _mybir.dt.from_np(a.dtype), kind="ExternalInput").ap())
    out = nc.dram_tensor("out", tuple(x.shape), F32, kind="ExternalOutput").ap()
    gat_kernel(nc, *args, out)
    r = _run(nc, [arrays], core_ids=[0])
    return r.results[0]["out"]
```
